# Optimizing a Trainium2 kernel written in Bass

```python
import numpy as np
import jax
import jax.numpy as jnp

def _softmax(x, axis=-1):
    return jax.nn.softmax(x, axis=axis)

def _gelu(x):
    return jax.nn.gelu(x, approximate=True)

def _silu(x):
    return jax.nn.silu(x)

def _sigmoid(x):
    return jax.nn.sigmoid(x)

def _layernorm(x, axis=-1, eps=1e-05):
    m = jnp.mean(x, axis=axis, keepdims=True)
    v = jnp.var(x, axis=axis, keepdims=True)
    return (x - m) / jnp.sqrt(v + eps)

def _scatter_add(tgt, idx, src, axis=0):
    return tgt.at[idx].add(src)

def _segment_sum(src, seg, n):
    return jax.ops.segment_sum(src, seg, n)
kernel_name = 'mk_macaron_d1_jaxref_r4_77d11f'

def setup_inputs(seed: int=0):
    np.random.seed(seed)
    _w = jnp.asarray

    def _L0_attn_setup():
        import jax, jax.numpy as jnp
        import numpy as np
        D_MODEL = 512
        N_HEAD = 16
        HEAD_DIM = D_MODEL // N_HEAD
        SCALE = 1.0 / HEAD_DIM ** 0.5
        key = jax.random.key(seed)
        kx, kq, kk, kv, ko = jax.random.split(key, 5)
        std = 1.0 / np.sqrt(D_MODEL)
        return {'x': jax.random.normal(kx, (2, 512, D_MODEL), dtype=jnp.float32), 'w_q': jax.random.normal(kq, (D_MODEL, D_MODEL), dtype=jnp.float32) * std, 'w_k': jax.random.normal(kk, (D_MODEL, D_MODEL), dtype=jnp.float32) * std, 'w_v': jax.random.normal(kv, (D_MODEL, D_MODEL), dtype=jnp.float32) * std, 'w_o': jax.random.normal(ko, (D_MODEL, D_MODEL), dtype=jnp.float32) * std}
    _L0_attn_in = _L0_attn_setup()

    def _L0_ffn_setup():
        import jax, jax.numpy as jnp
        import numpy as np

        @jax.custom_vjp
        def ste_sign(x):
            return jnp.sign(x)

        def _ste_fwd(x):
            return (jnp.sign(x), None)

        def _ste_bwd(_, g):
            return (g,)
        ste_sign.defvjp(_ste_fwd, _ste_bwd)
        D_MODEL = 512
        D_HIDDEN = 2048
        key = jax.random.key(seed)
        k_x, k_up, k_dn = jax.random.split(key, 3)
        x = jax.random.normal(k_x, (2, 512, D_MODEL), dtype=jnp.float32)
        up_weight = jax.random.normal(k_up, (D_HIDDEN, D_MODEL), dtype=jnp.float32) * 0.02
        down_weight = jax.random.normal(k_dn, (D_MODEL, D_HIDDEN), dtype=jnp.float32) * 0.02
        up_scale = jnp.ones((D_HIDDEN,), dtype=jnp.float32)
        down_scale = jnp.ones((D_MODEL,), dtype=jnp.float32)
        output_scale = jnp.ones((1,), dtype=jnp.float32)
        return {'x': x, 'up_weight': up_weight, 'down_weight': down_weight, 'up_scale': up_scale, 'down_scale': down_scale, 'output_scale': output_scale}
    _L0_ffn_in = _L0_ffn_setup()
    _d = {'L0_attn_x': _L0_attn_in['x'], 'L0_attn_w_q': _L0_attn_in['w_q'], 'L0_attn_w_k': _L0_attn_in['w_k'], 'L0_attn_w_v': _L0_attn_in['w_v'], 'L0_attn_w_o': _L0_attn_in['w_o'], 'L0_ffn_up_weight': _L0_ffn_in['up_weight'], 'L0_ffn_down_weight': _L0_ffn_in['down_weight'], 'L0_ffn_up_scale': _L0_ffn_in['up_scale'], 'L0_ffn_down_scale': _L0_ffn_in['down_scale'], 'L0_ffn_output_scale': _L0_ffn_in['output_scale']}
    _x0 = _d['L0_attn_x']
    _d['L0_attn_x'] = jax.random.normal(jax.random.fold_in(jax.random.key(seed), 1), (2, 2048, 512), dtype=_x0.dtype)
    del _x0
    return _d

def reference(L0_attn_x, L0_attn_w_q, L0_attn_w_k, L0_attn_w_v, L0_attn_w_o, L0_ffn_up_weight, L0_ffn_down_weight, L0_ffn_up_scale, L0_ffn_down_scale, L0_ffn_output_scale):

    def _L0_attn_ref(x, w_q, w_k, w_v, w_o):
        import jax, jax.numpy as jnp
        import numpy as np
        D_MODEL = 512
        N_HEAD = 16
        HEAD_DIM = D_MODEL // N_HEAD
        SCALE = 1.0 / HEAD_DIM ** 0.5
        b, s, d = x.shape

        def proj(w):
            y = jnp.einsum('bsd,ed->bse', x, w)
            return y.reshape(b, s, N_HEAD, HEAD_DIM).transpose(0, 2, 1, 3)
        q, k, v = (proj(w_q), proj(w_k), proj(w_v))
        scores = jnp.einsum('bhqd,bhkd->bhqk', q, k) * SCALE
        probs = jax.nn.softmax(scores, axis=-1)
        attn = jnp.einsum('bhqk,bhkd->bhqd', probs, v)
        attn = attn.transpose(0, 2, 1, 3).reshape(b, s, d)
        return jnp.einsum('bsd,ed->bse', attn, w_o)

    def _L0_ffn_ref(x, up_weight, down_weight, up_scale, down_scale, output_scale):
        import jax, jax.numpy as jnp
        import numpy as np

        @jax.custom_vjp
        def ste_sign(x):
            return jnp.sign(x)

        def _ste_fwd(x):
            return (jnp.sign(x), None)

        def _ste_bwd(_, g):
            return (g,)
        ste_sign.defvjp(_ste_fwd, _ste_bwd)
        D_MODEL = 512
        D_HIDDEN = 2048
        up_w = ste_sign(up_weight)
        down_w = ste_sign(down_weight)
        hidden = jnp.einsum('bsd,hd->bsh', x, up_w) * up_scale
        hidden = jax.nn.relu(hidden)
        out = jnp.einsum('bsh,dh->bsd', hidden, down_w) * down_scale
        return out * output_scale
    x = L0_attn_x
    x = x + 0.5 * _L0_ffn_ref(_layernorm(x, axis=-1), L0_ffn_up_weight, L0_ffn_down_weight, L0_ffn_up_scale, L0_ffn_down_scale, L0_ffn_output_scale)
    x = x + _L0_attn_ref(_layernorm(x, axis=-1), L0_attn_w_q, L0_attn_w_k, L0_attn_w_v, L0_attn_w_o)
    x = x + 0.5 * _L0_ffn_ref(_layernorm(x, axis=-1), L0_ffn_up_weight, L0_ffn_down_weight, L0_ffn_up_scale, L0_ffn_down_scale, L0_ffn_output_scale)
    return x

_drawn_inputs = setup_inputs


def setup_inputs(seed=0):
    import zlib

    import numpy as np

    out = dict(_drawn_inputs(seed))
    spreads = {'L0_ffn_up_scale': (1.0, 0.2), 'L0_ffn_down_scale': (1.0, 0.2)}
    factors = {'L0_attn_w_q': 8.0, 'L0_attn_w_k': 8.0, 'L0_attn_w_v': 8.0, 'L0_attn_w_o': 8.0}
    for name, (base, spread) in spreads.items():
        noise = np.random.default_rng([zlib.crc32(name.encode()), seed]).standard_normal(out[name].shape)
        drawn = base * np.exp(spread * noise) if base else spread * noise
        out[name] = jnp.asarray(drawn.astype(out[name].dtype))
    for name, factor in factors.items():
        out[name] = (out[name] * factor).astype(out[name].dtype)
    return out
```

```python
import concourse.bass as bass
from concourse import mybir
from contextlib import ExitStack

F32 = mybir.dt.float32
F32R = mybir.dt.float32r
ALU = mybir.AluOpType
ACT = mybir.ActivationFunctionType
AX = mybir.AxisListType

P = 128
BATCH, SEQ, D, HID = 2, 2048, 512, 2048
TOK = BATCH * SEQ
HEADS, HD = 16, 32
SCALE = 1.0 / HD ** 0.5
EPS = 1e-5
CH = 512
NCH = TOK // CH
DT = D // P
HT = HID // P
KT = SEQ // P
QC = SEQ // CH
NH = BATCH * HEADS

PARTS3 = ((0, 0), (0, 1), (1, 0))


def f32(ap):
    return ap.bitcast(F32)


NV, NA = 16, 3


class Norm:
    def __init__(self, nc, ctx, tag, ones_mean):
        def sb(n, shape, dt=F32):
            return ctx.enter_context(nc.sbuf_tensor(f"{tag}_{n}", shape, dt))
        self.nc, self.ones = nc, ones_mean
        self.pair = sb("pair", [P, 2, CH])
        self.sum = sb("sum", [P, CH])
        self.sum_hi, self.sum_lo = sb("sum_hi", [P, CH], F32R), sb("sum_lo", [P, CH], F32R)
        self.sq_hi, self.sq_lo = sb("sq_hi", [P, CH], F32R), sb("sq_lo", [P, CH], F32R)
        self.var, self.std = sb("var", [P, CH]), sb("std", [P, CH])
        self.inv, self.tmp = sb("inv", [P, CH]), sb("tmp", [P, CH])
        self.cent = sb("cent", [P, DT, CH])
        self.work = sb("work", [P, DT, CH])
        self.mean_ps = ctx.enter_context(nc.psum_tensor(f"{tag}_mean", [P, CH], F32))
        self.var_ps = ctx.enter_context(nc.psum_tensor(f"{tag}_varps", [P, CH], F32))
        self.dve = ctx.enter_context(nc.semaphore(f"{tag}_norm_dve"))
        self.act = ctx.enter_context(nc.semaphore(f"{tag}_norm_act"))
        self.pe = ctx.enter_context(nc.semaphore(f"{tag}_norm_pe"))

    def vector(self, dve, k, m, x, lo, hi):
        nc = self.nc
        if k not in (0, 4, 5, 9, 10, 15):
            dve.wait_ge(self.dve, m * NV + k)
        if k == 0:
            ins = nc.vector.tensor_tensor(self.pair[:], x[:, 0:2, :], x[:, 2:4, :], ALU.add)
        elif k == 1:
            ins = nc.vector.tensor_tensor(self.sum[:], self.pair[:, 0, :], self.pair[:, 1, :], ALU.add)
        elif k == 2:
            ins = nc.vector.tensor_copy(self.sum_hi[:], self.sum[:])
        elif k == 3:
            ins = nc.vector.tensor_tensor(self.sum_lo[:], self.sum[:], f32(self.sum_hi[:]), ALU.subtract)
        elif k == 4:
            dve.wait_ge(self.pe, m * 2 + 1)
            mean = self.mean_ps[:].unsqueeze(1).to_broadcast([P, DT, CH])
            ins = nc.vector.tensor_tensor(self.cent[:], x, mean, ALU.subtract)
        elif k == 5:
            dve.wait_ge(self.act, m * NA + 1)
            ins = nc.vector.tensor_tensor(self.pair[:], self.work[:, 0:2, :], self.work[:, 2:4, :], ALU.add)
        elif k == 6:
            ins = nc.vector.tensor_tensor(self.sum[:], self.pair[:, 0, :], self.pair[:, 1, :], ALU.add)
        elif k == 7:
            ins = nc.vector.tensor_copy(self.sq_hi[:], self.sum[:])
        elif k == 8:
            ins = nc.vector.tensor_tensor(self.sq_lo[:], self.sum[:], f32(self.sq_hi[:]), ALU.subtract)
        elif k == 9:
            dve.wait_ge(self.pe, m * 2 + 2)
            ins = nc.vector.tensor_scalar(self.var[:], self.var_ps[:], EPS, None, ALU.add)
        elif k == 10:
            dve.wait_ge(self.act, m * NA + 2)
            ins = nc.vector.reciprocal(self.inv[:], self.std[:])
        elif k == 11:
            ins = nc.vector.scalar_tensor_tensor(self.tmp[:], self.var[:], -0.5, self.inv[:], ALU.mult, ALU.mult)
        elif k == 12:
            ins = nc.vector.tensor_tensor(self.tmp[:], self.tmp[:], self.inv[:], ALU.mult)
        elif k == 13:
            ins = nc.vector.scalar_tensor_tensor(self.inv[:], self.tmp[:], 1.5, self.inv[:], ALU.add, ALU.mult)
        elif k == 14:
            inv = self.inv[:].unsqueeze(1).to_broadcast([P, DT, CH])
            ins = nc.vector.tensor_tensor(self.work[:], self.cent[:], inv, ALU.mult)
        elif k == 15:
            dve.wait_ge(self.act, m * NA + 3)
            ins = nc.vector.tensor_tensor(lo, self.work[:], f32(hi), ALU.subtract)
        ins.then_inc(self.dve, 1)

    def scalar(self, act, k, m, hi):
        nc = self.nc
        act.wait_ge(self.dve, m * NV + (5, 10, 15)[k])
        if k == 0:
            ins = nc.scalar.activation(self.work[:], self.cent[:], ACT.Square)
        elif k == 1:
            ins = nc.scalar.activation(self.std[:], self.var[:], ACT.Sqrt)
        else:
            ins = nc.scalar.activation(hi, self.work[:], ACT.Copy)
        ins.then_inc(self.act, 1)

    def tensor(self, pe, k, m):
        nc = self.nc
        pe.wait_ge(self.dve, m * NV + (4, 9)[k])
        out = (self.mean_ps, self.var_ps)[k]
        hi, lo = ((self.sum_hi, self.sum_lo), (self.sq_hi, self.sq_lo))[k]
        nc.tensor.matmul(out[:], self.ones[:], hi[:], start=True, stop=False)
        nc.tensor.matmul(out[:], self.ones[:], lo[:], start=False, stop=True).then_inc(self.pe, 1)


def chunk(ap, n):
    return ap[:, :, bass.ds(n * CH, CH)]


def ffn_phase(nc, tag, x_in, x_out, up_raw, down_raw, vecs, ones_mean):
    with ExitStack() as ctx:
        def sb(n, shape, dt=F32):
            return ctx.enter_context(nc.sbuf_tensor(f"{tag}_{n}", shape, dt))

        def ps(n):
            return ctx.enter_context(nc.psum_tensor(f"{tag}_{n}", [P, CH], F32))

        def sem(n):
            return ctx.enter_context(nc.semaphore(f"{tag}_{n}"))

        up_w = sb("up_w", [P, DT, HID], F32R)
        down_w = sb("down_w", [P, HT, D], F32R)
        x = [sb(f"x{i}", [P, DT, CH]) for i in range(2)]
        xh = [sb(f"xh{i}", [P, DT, CH], F32R) for i in range(2)]
        xl = [sb(f"xl{i}", [P, DT, CH], F32R) for i in range(2)]
        RING, RAW = 4, 2
        hid_hi, hid_lo = sb("hid_hi", [P, RING, CH], F32R), sb("hid_lo", [P, RING, CH], F32R)
        hid = sb("hid", [P, RAW, CH])
        norm = Norm(nc, ctx, tag, ones_mean)
        up_ps = [ps(f"up{i}") for i in range(2)]
        down_ps = [ps(f"down{i}") for i in range(DT)]

        x_loaded = [sem(f"x_loaded{i}") for i in range(2)]
        x_stored = [sem(f"x_stored{i}") for i in range(2)]
        w_loaded = [sem(f"w_loaded{i}") for i in range(4)]
        w_neg, w_sign = sem("w_neg"), sem("w_sign")
        up_ready = sem("up_ready")
        up_read = sem("up_read")
        hid_ready = sem("hid_ready")
        hid_used = sem("hid_used")
        down_read = sem("down_read")
        LAG = 3

        with nc.Block() as block:
            NP = NCH // 2

            def xstage(q):
                return (norm.cent if q % 2 == 0 else norm.work)[:].rearrange("p a b -> p (a b)")

            @block.sync
            def _(sp):
                for q in range(4):
                    if q >= 2:
                        sp.wait_ge(w_sign, 2 * (q - 1))
                    sp.dma_start(xstage(q), up_raw[:, q, :]).then_inc(w_loaded[q], 16)
                for q in range(4):
                    sp.wait_ge(w_sign, 2 * (q + 3))
                    sp.dma_start(xstage(q), down_raw[:, 4 * q:4 * q + 4, :].rearrange("p a b -> p (a b)")).then_inc(w_loaded[q], 16)
                for i in range(2):
                    sp.dma_start(x[i][:], chunk(x_in, i)).then_inc(x_loaded[i], 16)

                def pair(cp, last):
                    for j in range(2):
                        sp.wait_ge(down_read, 2 * cp + j + 2)
                        sp.dma_start(chunk(x_out, 2 * cp + j), x[j][:]).then_inc(x_stored[j], 16)
                        if not last:
                            sp.wait_ge(x_stored[j], 16 * cp + 16)
                            sp.dma_start(x[j][:], chunk(x_in, 2 * cp + j + 2)).then_inc(x_loaded[j], 16)
                with sp.Fori(0, NP - 1) as cp:
                    pair(cp, False)
                pair(NP - 1, True)
                for j in range(2):
                    sp.wait_ge(x_stored[j], 16 * NP)

            DVE_AT = {0: (0, 1), 1: (2, 3), 5: (4,), 7: (5, 6), 8: (7, 8), 11: (9,), 12: (10,),
                      13: (11, 12, 13), 14: (14,), 15: (15,)}
            ACT_AT = {5: 0, 11: 1, 14: 2}
            PE_AT = {3: 0, 10: 1}

            @block.vector
            def _(dve):
                dve.sem_inc(hid_ready, RAW)
                dve.sem_inc(down_read, 1)
                for q in range(8):
                    dve.wait_ge(w_loaded[q % 4], 16 * (q // 4 + 1))
                    st = xstage(q)
                    dst = up_w[:, q, :] if q < 4 else down_w[:, 4 * (q - 4):4 * (q - 3), :].rearrange("p a b -> p (a b)")
                    if q:
                        dve.wait_ge(w_sign, 2 * q)
                    nc.vector.tensor_scalar(dst, st, 0.0, None, ALU.is_lt).then_inc(w_sign, 1)
                    dve.wait_ge(w_sign, 2 * q + 1)
                    nc.vector.scalar_tensor_tensor(dst, st, 0.0, f32(dst), ALU.is_gt, ALU.subtract).then_inc(w_sign, 1)
                dve.wait_ge(w_sign, 16)
                dve.wait_ge(x_loaded[0], 16)
                for k in range(NV):
                    norm.vector(dve, k, 0, x[0][:], xl[0][:], xh[0][:])

                def pair(cp, last):
                    for j in range(2):
                        n = 2 * cp + j
                        for ht in range(HT):
                            dve.wait_ge(up_read, 2 + n * HT + ht + 1)
                            nc.vector.tensor_tensor(hid_lo[:, ht % RING, :], hid[:, ht % RAW, :],
                                                    f32(hid_hi[:, ht % RING, :]), ALU.subtract).then_inc(hid_ready, 1)
                            if not (last and j):
                                if ht == 0:
                                    dve.wait_ge(x_loaded[1 - j], 16 * (cp + j) + 16)
                                for k in DVE_AT.get(ht, ()):
                                    norm.vector(dve, k, n + 1, x[1 - j][:], xl[1 - j][:], xh[1 - j][:])
                        dve.wait_ge(hid_used, RING + n * HT + HT)
                        for dt in range(DT):
                            ins = nc.vector.scalar_tensor_tensor(x[j][:, dt, :], down_ps[dt][:], vecs["down"][:, dt:dt + 1],
                                                                 x[j][:, dt, :], ALU.mult, ALU.add)
                        ins.then_inc(down_read, 1)
                with dve.Fori(0, NP - 1) as cp:
                    pair(cp, False)
                pair(NP - 1, True)

            @block.scalar
            def _(act):
                act.sem_inc(up_read, 2)
                for k in range(NA):
                    norm.scalar(act, k, 0, xh[0][:])

                def pair(cp, last):
                    for j in range(2):
                        n = 2 * cp + j
                        for ht in range(HT):
                            act.wait_ge(up_ready, n * HT + ht + 1)
                            act.wait_ge(hid_ready, n * HT + ht + 1)
                            nc.scalar.activation(hid[:, ht % RAW, :], up_ps[ht % 2][:], ACT.Relu,
                                                 scale=vecs["up"][:, ht:ht + 1])
                            act.wait_ge(hid_used, n * HT + ht + 1)
                            nc.scalar.activation(hid_hi[:, ht % RING, :], up_ps[ht % 2][:], ACT.Relu,
                                                 scale=vecs["up"][:, ht:ht + 1]).then_inc(up_read, 1)
                            if ht in ACT_AT and not (last and j):
                                norm.scalar(act, ACT_AT[ht], n + 1, xh[1 - j][:])
                with act.Fori(0, NP - 1) as cp:
                    pair(cp, False)
                pair(NP - 1, True)

            @block.tensor
            def _(pe):
                pe.sem_inc(hid_used, RING)
                norm.tensor(pe, 0, 0)
                norm.tensor(pe, 1, 0)
                pe.wait_ge(w_sign, 16)

                def pair(cp, last):
                    for j in range(2):
                        n = 2 * cp + j
                        pe.wait_ge(norm.dve, NV * (n + 1))
                        for ht in range(HT + LAG):
                            if ht < HT:
                                pe.wait_ge(up_read, n * HT + ht + 1)
                                for dt in range(DT):
                                    for part in (xh, xl):
                                        ins = nc.tensor.matmul(up_ps[ht % 2][:], up_w[:, dt, ht * P:(ht + 1) * P],
                                                               part[j][:, dt, :], start=(dt == 0 and part is xh),
                                                               stop=(dt == DT - 1 and part is xl))
                                ins.then_inc(up_ready, 1)
                            if ht in PE_AT and not (last and j):
                                norm.tensor(pe, PE_AT[ht], n + 1)
                            h = ht - LAG
                            if h >= 0:
                                if h == 0:
                                    pe.wait_ge(down_read, n + 1)
                                pe.wait_ge(hid_ready, RAW + n * HT + h + 1)
                                for dt in range(DT):
                                    for part in (hid_hi, hid_lo):
                                        ins = nc.tensor.matmul(down_ps[dt][:], down_w[:, h, dt * P:(dt + 1) * P],
                                                               part[:, h % RING, :], start=(h == 0 and part is hid_hi),
                                                               stop=(h == HT - 1 and part is hid_lo))
                                ins.then_inc(hid_used, 1)
                with pe.Fori(0, NP - 1) as cp:
                    pair(cp, False)
                pair(NP - 1, True)


def qkv_phase(nc, x_in, w_raw, qk_parts, v_scr, ones_mean):
    with ExitStack() as ctx:
        def sb(n, shape, dt=F32):
            return ctx.enter_context(nc.sbuf_tensor(f"qkv_{n}", shape, dt))

        def sem(n):
            return ctx.enter_context(nc.semaphore(f"qkv_{n}"))

        w_hi, w_lo = sb("w_hi", [P, 3, DT, D], F32R), sb("w_lo", [P, 3, DT, D], F32R)
        w_st = sb("w_st", [P, DT, D])
        x = [sb(f"x{i}", [P, DT, CH]) for i in range(2)]
        xh = [sb(f"xh{i}", [P, DT, CH], F32R) for i in range(2)]
        xl = [sb(f"xl{i}", [P, DT, CH], F32R) for i in range(2)]
        norm = Norm(nc, ctx, "qkv", ones_mean)
        RING = 4
        o_hi, o_lo = sb("o_hi", [P, RING, CH], F32R), sb("o_lo", [P, RING, CH], F32R)
        o_v = sb("o_v", [P, RING, CH])
        out_ps = [ctx.enter_context(nc.psum_tensor(f"qkv_o{i}", [P, CH], F32)) for i in range(RING)]
        x_loaded = [sem(f"x_loaded{i}") for i in range(2)]
        w_loaded, w_split = sem("w_loaded"), sem("w_split")
        out_ready = sem("out_ready")
        act_read = sem("act_read")
        out_read = sem("out_read")
        stored = [sem(f"stored{i}") for i in range(RING)]
        NT = 12
        PER = 80
        BEFORE = (16, 48, 80)

        with nc.Block() as block:
            @block.sync
            def _(sp):
                for s in range(RING):
                    sp.sem_inc(stored[s], 16)
                for i in range(2):
                    sp.dma_start(x[i][:], chunk(x_in, i)).then_inc(x_loaded[i], 16)
                for w in range(3):
                    if w:
                        sp.wait_ge(w_split, 2 * w)
                    sp.dma_start(w_st[:], w_raw[w]).then_inc(w_loaded, 16)

                def pair(cp, last):
                    for j in range(2):
                        n = 2 * cp + j
                        for t in range(NT):
                            sp.wait_ge(out_read, RING + n * NT + t + 1)
                            s = t % RING
                            if t < 8:
                                rows = slice((t % 4) * P, (t % 4 + 1) * P)
                                for part, src in ((0, o_hi), (1, o_lo)):
                                    dst = qk_parts[t // 4][part][rows, bass.ds(n * CH, CH)]
                                    sp.dma_start(dst, f32(src[:, s, :])).then_inc(stored[s], 16)
                            else:
                                sp.dma_start(v_scr[bass.ds(n * CH + (t - 8) * P, P), :], o_v[:, s, :]).then_inc(stored[s], 16)
                        if not last:
                            sp.wait_ge(norm.dve, NV * (n + 1))
                            sp.dma_start(x[j][:], chunk(x_in, n + 2)).then_inc(x_loaded[j], 16)
                with sp.Fori(0, NCH // 2 - 1) as cp:
                    pair(cp, False)
                pair(NCH // 2 - 1, True)
                for s in range(RING):
                    sp.wait_ge(stored[s], PER * NCH + 16)

            DVE_AT = {0: (0, 1, 2, 3), 3: (4,), 5: (5, 6, 7, 8), 7: (9,), 8: (10,), 9: (11, 12, 13, 14), 11: (15,)}
            ACT_AT = {3: 0, 7: 1, 10: 2}
            PE_AT = {2: 0, 7: 1}

            @block.vector
            def _(dve):
                dve.sem_inc(out_read, RING)
                dve.wait_ge(x_loaded[0], 16)
                for w in range(3):
                    dve.wait_ge(w_loaded, 16 * w + 16)
                    nc.vector.tensor_copy(w_hi[:, w], w_st[:]).then_inc(w_split, 1)
                    dve.wait_ge(w_split, 2 * w + 1)
                    nc.vector.tensor_tensor(w_lo[:, w], w_st[:], f32(w_hi[:, w]), ALU.subtract).then_inc(w_split, 1)
                for k in range(NV):
                    norm.vector(dve, k, 0, x[0][:], xl[0][:], xh[0][:])

                def pair(cp, last):
                    for j in range(2):
                        n = 2 * cp + j
                        for t in range(NT):
                            s = t % RING
                            if t < 8:
                                dve.wait_ge(act_read, n * 8 + t + 1)
                                nc.vector.tensor_tensor(o_lo[:, s, :], out_ps[s][:], f32(o_hi[:, s, :]),
                                                        ALU.subtract).then_inc(out_read, 1)
                            else:
                                dve.wait_ge(stored[s], n * PER + BEFORE[2])
                                dve.wait_ge(out_ready, n * NT + t + 1)
                                nc.vector.tensor_copy(o_v[:, s, :], out_ps[s][:]).then_inc(out_read, 1)
                            if not (last and j):
                                if t == 0:
                                    dve.wait_ge(x_loaded[1 - j], 16 * (cp + j) + 16)
                                for k in DVE_AT.get(t, ()):
                                    norm.vector(dve, k, n + 1, x[1 - j][:], xl[1 - j][:], xh[1 - j][:])
                with dve.Fori(0, NCH // 2 - 1) as cp:
                    pair(cp, False)
                pair(NCH // 2 - 1, True)

            @block.scalar
            def _(act):
                for k in range(NA):
                    norm.scalar(act, k, 0, xh[0][:])

                def pair(cp, last):
                    for j in range(2):
                        n = 2 * cp + j
                        for t in range(NT):
                            s = t % RING
                            if t < 8:
                                act.wait_ge(stored[s], n * PER + BEFORE[t // 4])
                                act.wait_ge(out_ready, n * NT + t + 1)
                                nc.scalar.activation(o_hi[:, s, :], out_ps[s][:], ACT.Copy).then_inc(act_read, 1)
                            if t in ACT_AT and not (last and j):
                                norm.scalar(act, ACT_AT[t], n + 1, xh[1 - j][:])
                with act.Fori(0, NCH // 2 - 1) as cp:
                    pair(cp, False)
                pair(NCH // 2 - 1, True)

            @block.tensor
            def _(pe):
                norm.tensor(pe, 0, 0)
                norm.tensor(pe, 1, 0)
                pe.wait_ge(w_split, 6)
                w = (w_hi, w_lo)

                def pair(cp, last):
                    for j in range(2):
                        n = 2 * cp + j
                        act_parts = (xh[j], xl[j])
                        pe.wait_ge(norm.dve, NV * (n + 1))
                        for t in range(NT):
                            pe.wait_ge(out_read, n * NT + t + 1)
                            which, i = t // 4, t % 4
                            for dt in range(DT):
                                for a, b in PARTS3:
                                    if which < 2:
                                        left, right = w[a][:, which, dt, i * P:(i + 1) * P], act_parts[b][:, dt, :]
                                    else:
                                        left, right = act_parts[b][:, dt, i * P:(i + 1) * P], w[a][:, which, dt, :]
                                    ins = nc.tensor.matmul(out_ps[t % RING][:], left, right,
                                                           start=(dt == 0 and (a, b) == (0, 0)),
                                                           stop=(dt == DT - 1 and (a, b) == (1, 0)))
                            ins.then_inc(out_ready, 1)
                            if t in PE_AT and not (last and j):
                                norm.tensor(pe, PE_AT[t], n + 1)
                with pe.Fori(0, NCH // 2 - 1) as cp:
                    pair(cp, False)
                pair(NCH // 2 - 1, True)


def attention_phase(nc, qk_parts, v_scr, att, sums_scr, inv_scr, ident, ones_sum):
    NB = 4
    KQ, KM = 3 * HD, 3 * HD + 2
    LEAD, LAG = 3, 2
    PR = 8
    SR, MR = 4, 2
    POOLED = (0, 1, 3, 4, 6, 7, 9, 10, 12, 13)
    NA_ = len(POOLED) - 1
    PER = 7 * 16
    with ExitStack() as ctx:
        def sb(n, shape, dt=F32):
            return ctx.enter_context(nc.sbuf_tensor(f"att_{n}", shape, dt))

        def ps(n):
            return ctx.enter_context(nc.psum_tensor(f"att_{n}", [P, CH], F32))

        def sem(n):
            return ctx.enter_context(nc.semaphore(f"att_{n}"))

        q_st = [sb(f"q{i}", [P, SEQ], F32R) for i in range(NB)]
        k_st = [sb(f"k{i}", [P, SEQ], F32R) for i in range(NB)]
        v_st = [sb(f"v{i}", [P, KT, HD]) for i in range(NB)]
        prob = [sb(f"p{i}", [P, SEQ]) for i in range(PR)]
        acc = [sb(f"acc{i}", [P, SEQ]) for i in range(2)]
        row_max = sb("row_max", [P, KT, QC])
        neg_max = sb("neg_max", [P, KT])
        neg_parts = sb("neg_parts", [P, 2, KT], F32R)
        neg_rows = sb("neg_rows", [2 * KT, P], F32R)
        un, total = sb("un", [P, CH]), sb("total", [P, CH])
        tot_t, inv_t = sb("tot_t", [P, KT]), sb("inv_t", [P, KT])
        inv_b, fin = sb("inv_b", [P, CH]), sb("fin", [P, CH])
        s_ps = [ps(f"s{i}") for i in range(SR)]
        m_ps = [ps(f"m{i}") for i in range(MR)]
        o_ps, t_ps = ps("o"), ps("t")

        loaded = [sem(f"loaded{i}") for i in range(NB)]
        ones_set = sem("ones_set")
        m_ready, m_read = sem("m_ready"), sem("m_read")
        neg_dve, neg_pe = sem("neg_dve"), sem("neg_pe")
        neg_loaded = sem("neg_loaded")
        s_ready, exp_done = sem("s_ready"), sem("exp_done")
        p_used = sem("p_used")
        summed = sem("summed")
        t_ready, evac = sem("t_ready"), sem("evac")
        tail = sem("tail")
        div = sem("div")

        def adds_before(kt):
            return max(1, POOLED.index(kt))

        with nc.Block() as block:
            def groups(eng, body):
                body(0, True, False)
                with eng.Fori(1, NH // NB - 1) as g:
                    body(g, False, False)
                body(NH // NB - 1, False, True)

            @block.sync
            def _(sp):
                def load(b, row, col):
                    for which, st in ((0, q_st[b]), (1, k_st[b])):
                        for i, part in enumerate(((0, 0, 1), (0, 1, 0))[which]):
                            sp.dma_start(f32(st[i * HD:(i + 1) * HD, :]),
                                         qk_parts[which][part][bass.ds(row, HD), bass.ds(col, SEQ)]).then_inc(loaded[b], 16)
                    sp.dma_start(v_st[b][:], v_scr[bass.ds(col, SEQ), bass.ds(row, HD)].rearrange("(t p) d -> p t d", p=P)
                                 ).then_inc(loaded[b], 16)

                def max_rows(b, H):
                    sp.wait_ge(neg_dve, 4 * H + 4)
                    for r in range(2):
                        sp.dma_start(f32(q_st[b][KQ + r:KQ + r + 1, :].rearrange("o (t p) -> o t p", p=P)),
                                     f32(neg_rows[r * KT:(r + 1) * KT, :])).then_inc(neg_loaded, 16)

                def normalise(H, row, col):
                    T = 11 * 16
                    sp.wait_ge(evac, 2 * H + 2)
                    sp.dma_start(sums_scr[:, :], total[0:P:HD, :]).then_inc(tail, 16)
                    sp.wait_ge(tail, T * H + 16)
                    sp.dma_start(tot_t[:], sums_scr.rearrange("a (b c) -> (a b) c", c=KT)).then_inc(tail, 16)
                    sp.wait_ge(div, 2 * H + 1)
                    sp.dma_start(inv_scr.rearrange("a (b c) -> (a b) c", c=KT), inv_t[:]).then_inc(tail, 16)
                    sp.wait_ge(tail, T * H + 48)
                    for c in range(QC):
                        sp.dma_start(inv_b[c * HD:(c + 1) * HD, :], inv_scr[c:c + 1, :].to_broadcast([HD, CH])).then_inc(tail, 16)
                    sp.wait_ge(div, 2 * H + 2)
                    for c in range(QC):
                        sp.dma_start(att[bass.ds(row, HD), bass.ds(col + c * CH, CH)], fin[c * HD:(c + 1) * HD, :]).then_inc(tail, 16)

                for b in range(3):
                    load(b, b * HD, 0)
                max_rows(0, 0)

                def body(g, first, last):
                    for j in range(NB):
                        H = NB * g + j
                        if not (last and j):
                            sp.wait_ge(s_ready, 64 * H)
                            sp.wait_ge(p_used, PR + KT * H)
                            X = H + 3
                            load((j + 3) % NB, X % HEADS * HD, X // HEADS * SEQ)
                        if not (first and j == 0):
                            Y = H - 1
                            normalise(Y, Y % HEADS * HD, Y // HEADS * SEQ)
                        if not (last and j == NB - 1):
                            max_rows((j + 1) % NB, H + 1)
                groups(sp, body)
                normalise(NH - 1, (HEADS - 1) * HD, SEQ)
                sp.wait_ge(tail, 11 * 16 * NH)

            @block.gpsimd
            def _(pool):
                for b in range(NB):
                    nc.gpsimd.memset(f32(k_st[b][KQ:KM, :]), 1.0).then_inc(ones_set, 1)
                pool.sem_inc(summed, NA_)

                def body(g, first, last):
                    for j in range(NB):
                        H = NB * g + j
                        for i, kt in enumerate(POOLED):
                            if i == 0:
                                continue
                            pool.wait_ge(exp_done, SR + 64 * H + 4 * kt + 4)
                            if i == 1:
                                if not (first and j < 2):
                                    pool.wait_ge(t_ready, H - 1)
                                a = prob[POOLED[0] % PR]
                            else:
                                pool.wait_ge(summed, NA_ * (H + 1) + i - 1)
                                a = acc[j % 2]
                            nc.gpsimd.tensor_tensor(acc[j % 2][:], a[:], prob[kt % PR][:], ALU.add).then_inc(summed, 1)
                groups(pool, body)

            @block.vector
            def _(dve):
                dve.sem_inc(m_read, MR)

                def reduce_tile(T, qt):
                    for c in range(QC):
                        dve.wait_ge(m_ready, QC * T + c + 1)
                        nc.vector.tensor_reduce(row_max[:, qt, c:c + 1], m_ps[c % MR][:], axis=AX.X, op=ALU.max).then_inc(m_read, 1)

                def negate(T_end, h):
                    dve.wait_ge(m_read, MR + QC * T_end)
                    nc.vector.tensor_reduce(neg_max[:], row_max[:], axis=AX.X, op=ALU.max, negate=True).then_inc(neg_dve, 1)
                    dve.wait_ge(neg_dve, 4 * h + 1)
                    nc.vector.tensor_copy(neg_parts[:, 0, :], neg_max[:]).then_inc(neg_dve, 1)
                    dve.wait_ge(neg_dve, 4 * h + 2)
                    nc.vector.tensor_tensor(neg_parts[:, 1, :], neg_max[:], f32(neg_parts[:, 0, :]), ALU.subtract).then_inc(neg_dve, 1)

                def rows_out(h, wait):
                    dve.wait_ge(neg_pe, h + 1)
                    if wait:
                        dve.wait_ge(neg_loaded, 32 * h)
                    nc.vector.tensor_copy(neg_rows[:], m_ps[0][0:2 * KT, 0:P]).then_inc(neg_dve, 1)

                T = 0
                for qt in range(KT):
                    reduce_tile(qt, qt)
                negate(KT, 0)
                rows_out(0, False)
                for qt in range(LEAD):
                    reduce_tile(KT + qt, qt)

                def body(g, first, last):
                    for j in range(NB):
                        H = NB * g + j
                        for kt in range(KT):
                            step_max = not (last and (j == NB - 1 or (j == NB - 2 and kt + LEAD >= KT)))
                            qt = (kt + LEAD) % KT
                            if kt == KT - LEAD and not (last and j == NB - 1):
                                rows_out(H + 1, True)
                            if step_max:
                                reduce_tile(KT * (H + 1) + kt + LEAD, qt)
                                if qt == KT - 1:
                                    negate(KT * (H + 2), H + 1)
                            if not (first and j == 0):
                                if kt == 7:
                                    dve.wait_ge(tail, 176 * (H - 1) + 32)
                                    nc.vector.reciprocal(inv_t[:], tot_t[:]).then_inc(div, 1)
                                if kt == 12:
                                    dve.wait_ge(tail, 176 * (H - 1) + 112)
                                    nc.vector.tensor_tensor(fin[:], un[:], inv_b[:], ALU.mult).then_inc(div, 1)
                groups(dve, body)
                dve.wait_ge(tail, 176 * (NH - 1) + 32)
                nc.vector.reciprocal(inv_t[:], tot_t[:]).then_inc(div, 1)
                dve.wait_ge(tail, 176 * (NH - 1) + 112)
                nc.vector.tensor_tensor(fin[:], un[:], inv_b[:], ALU.mult).then_inc(div, 1)

            @block.scalar
            def _(act):
                act.sem_inc(exp_done, SR)

                def copy_out(H):
                    act.wait_ge(p_used, PR + KT * H + KT)
                    if not isinstance(H, int) or H > 0:
                        act.wait_ge(div, 2 * H)
                    nc.scalar.activation(un[:], o_ps[:], ACT.Copy).then_inc(evac, 1)

                def copy_sums(H):
                    act.wait_ge(t_ready, H + 1)
                    if not isinstance(H, int) or H > 0:
                        act.wait_ge(tail, 176 * (H - 1) + 32)
                    nc.scalar.activation(total[:], t_ps[:], ACT.Copy).then_inc(evac, 1)

                def body(g, first, last):
                    for j in range(NB):
                        H = NB * g + j
                        for kt in range(KT):
                            if not (first and j == 0):
                                if kt == LAG:
                                    copy_out(H - 1)
                                if kt == LAG + 2:
                                    copy_sums(H - 1)
                            act.wait_ge(p_used, KT * H + kt + 1)
                            old = (kt - PR) % KT
                            if old in POOLED:
                                h_old = H if kt >= PR else H - 1
                                act.wait_ge(summed, NA_ * (h_old + 1) + adds_before(old))
                            for c in range(QC):
                                act.wait_ge(s_ready, 64 * H + 4 * kt + c + 1)
                                nc.scalar.activation(prob[kt % PR][:, c * CH:(c + 1) * CH], s_ps[c][:], ACT.Exp,
                                                     scale=SCALE).then_inc(exp_done, 1)
                groups(act, body)
                copy_out(NH - 1)
                copy_sums(NH - 1)

            @block.tensor
            def _(pe):
                pe.sem_inc(p_used, PR)
                pe.wait_ge(ones_set, NB)

                def maxima(b, T, qt, c):
                    pe.wait_ge(m_read, QC * T + c + 1)
                    nc.tensor.matmul(m_ps[c % MR][:], q_st[b][0:KQ, qt * P:(qt + 1) * P], k_st[b][0:KQ, c * CH:(c + 1) * CH],
                                     start=True, stop=True).then_inc(m_ready, 1)

                def transpose_max(h):
                    pe.wait_ge(neg_dve, 4 * h + 3)
                    nc.tensor.transpose(m_ps[0][0:2 * KT, 0:P], f32(neg_parts[:].rearrange("p a b -> p (a b)")),
                                        ident[:]).then_inc(neg_pe, 1)

                def out_tile(H, b, kt):
                    pe.wait_ge(exp_done, SR + 64 * H + 4 * kt + 4)
                    if kt == 0 and not (isinstance(H, int) and H == 0):
                        pe.wait_ge(evac, 2 * H - 1)
                    for c in range(QC):
                        rows = slice(c * HD, (c + 1) * HD)
                        ins = nc.tensor.matmul(o_ps[rows, :], v_st[b][:, kt, :], prob[kt % PR][:, c * CH:(c + 1) * CH],
                                               start=(kt == 0), stop=(kt == KT - 1))
                    if kt not in POOLED:
                        if kt == 2 and not (isinstance(H, int) and H == 0):
                            pe.wait_ge(evac, 2 * H)
                        for c in range(QC):
                            rows = slice(c * HD, (c + 1) * HD)
                            ins = nc.tensor.matmul(t_ps[rows, :], ones_sum[:], prob[kt % PR][:, c * CH:(c + 1) * CH],
                                                   start=(kt == 2), stop=False)
                    ins.then_inc(p_used, 1)

                def pooled_sums(H, b2):
                    pe.wait_ge(summed, NA_ * (H + 2))
                    for c in range(QC):
                        rows = slice(c * HD, (c + 1) * HD)
                        ins = nc.tensor.matmul(t_ps[rows, :], ones_sum[:], acc[b2][:, c * CH:(c + 1) * CH],
                                               start=False, stop=True)
                    ins.then_inc(t_ready, 1)

                pe.wait_ge(loaded[0], PER)
                for qt in range(KT):
                    for c in range(QC):
                        maxima(0, qt, qt, c)
                transpose_max(0)
                pe.wait_ge(loaded[1], PER)
                pe.wait_ge(neg_dve, 4)
                for qt in range(LEAD):
                    for c in range(QC):
                        maxima(1, KT + qt, qt, c)

                def body(g, first, last):
                    for j in range(NB):
                        H = NB * g + j
                        pe.wait_ge(neg_loaded, 32 * (H + 1))
                        for kt in range(KT):
                            step_max = not (last and (j == NB - 1 or (j == NB - 2 and kt + LEAD >= KT)))
                            late = kt == KT - LEAD
                            b, qt = ((j + 1) % NB, kt + LEAD) if kt + LEAD < KT else ((j + 2) % NB, kt + LEAD - KT)
                            T = KT * (H + 1) + kt + LEAD
                            for c in range(QC):
                                pe.wait_ge(exp_done, 64 * H + 4 * kt + c + 1)
                                nc.tensor.matmul(s_ps[c][:], k_st[j][0:KM, kt * P:(kt + 1) * P],
                                                 q_st[j][0:KM, c * CH:(c + 1) * CH], start=True, stop=True).then_inc(s_ready, 1)
                                if step_max and not late:
                                    maxima(b, T, qt, c)
                            if late and not (last and j == NB - 1):
                                transpose_max(H + 1)
                            if kt >= LAG:
                                out_tile(H, j, kt - LAG)
                            elif not (first and j == 0):
                                out_tile(H - 1, (j - 1) % NB, KT + kt - LAG)
                            if kt == LAG + 1 and not (first and j == 0):
                                pooled_sums(H - 1, (j - 1) % 2)
                            if step_max and late:
                                pe.wait_ge(loaded[b], PER * (g + 1 + (j + 2) // NB))
                                pe.wait_ge(neg_dve, 4 * (H + 1) + 4)
                                for c in range(QC):
                                    maxima(b, T, qt, c)
                groups(pe, body)
                for kt in range(KT - LAG, KT):
                    out_tile(NH - 1, NB - 1, kt)
                pooled_sums(NH - 1, (NH - 1) % 2)


def oproj_phase(nc, att, x_in, w_raw, x_out):
    with ExitStack() as ctx:
        def sb(n, shape, dt=F32):
            return ctx.enter_context(nc.sbuf_tensor(f"op_{n}", shape, dt))

        def sem(n):
            return ctx.enter_context(nc.semaphore(f"op_{n}"))

        w_st = sb("w_st", [P, DT, D])
        w = (sb("w_hi", [P, DT, D], F32R), sb("w_lo", [P, DT, D], F32R))
        a = [sb(f"a{i}", [P, DT, CH]) for i in range(2)]
        parts = [(sb(f"ah{i}", [P, DT, CH], F32R), sb(f"al{i}", [P, DT, CH], F32R)) for i in range(2)]
        x = [sb(f"x{i}", [P, DT, CH]) for i in range(2)]
        out_ps = [[ctx.enter_context(nc.psum_tensor(f"op_o{i}_{t}", [P, CH], F32)) for t in range(DT)] for i in range(2)]
        w_loaded, w_split = sem("w_loaded"), sem("w_split")
        a_loaded = [sem(f"a_loaded{i}") for i in range(2)]
        x_loaded = [sem(f"x_loaded{i}") for i in range(2)]
        x_stored = [sem(f"x_stored{i}") for i in range(2)]
        hi_done, lo_done = sem("hi_done"), sem("lo_done")
        ready, added = sem("ready"), sem("added")

        with nc.Block() as block:
            @block.sync
            def _(sp):
                sp.dma_start(w_st[:], w_raw).then_inc(w_loaded, 16)

                def load(j, n):
                    sp.dma_start(a[j][:], chunk(att, n)).then_inc(a_loaded[j], 16)
                    sp.dma_start(x[j][:], chunk(x_in, n)).then_inc(x_loaded[j], 16)
                load(0, 0)
                load(1, 1)

                def pair(cp, last):
                    for j in range(2):
                        n = 2 * cp + j
                        sp.wait_ge(added, n + 3)
                        sp.dma_start(chunk(x_out, n), x[j][:]).then_inc(x_stored[j], 16)
                        if not last:
                            sp.wait_ge(x_stored[j], 16 * cp + 16)
                            load(j, n + 2)
                with sp.Fori(0, NCH // 2 - 1) as cp:
                    pair(cp, False)
                pair(NCH // 2 - 1, True)
                for j in range(2):
                    sp.wait_ge(x_stored[j], 16 * (NCH // 2))

            @block.scalar
            def _(act):
                with act.Fori(0, NCH // 2) as cp:
                    for j in range(2):
                        n = 2 * cp + j
                        act.wait_ge(a_loaded[j], 16 * cp + 16)
                        act.wait_ge(ready, 2 * cp + 2)
                        nc.scalar.activation(parts[j][0][:], a[j][:], ACT.Copy).then_inc(hi_done, 1)

            @block.vector
            def _(dve):
                dve.sem_inc(added, 2)
                dve.wait_ge(w_loaded, 16)
                nc.vector.tensor_copy(w[0][:], w_st[:]).then_inc(w_split, 1)
                dve.wait_ge(w_split, 1)
                nc.vector.tensor_tensor(w[1][:], w_st[:], f32(w[0][:]), ALU.subtract).then_inc(w_split, 1)

                def split(j, n):
                    dve.wait_ge(hi_done, n + 1)
                    nc.vector.tensor_tensor(parts[j][1][:], a[j][:], f32(parts[j][0][:]), ALU.subtract).then_inc(lo_done, 1)

                def pair(cp, last):
                    for j in range(2):
                        n = 2 * cp + j
                        if not (last and j):
                            split(1 - j, n + 1)
                        dve.wait_ge(x_loaded[j], 16 * cp + 16)
                        dve.wait_ge(ready, n + 3)
                        for t in range(DT):
                            ins = nc.vector.tensor_tensor(x[j][:, t, :], out_ps[j][t][:], x[j][:, t, :], ALU.add)
                        ins.then_inc(added, 1)
                split(0, 0)
                with dve.Fori(0, NCH // 2 - 1) as cp:
                    pair(cp, False)
                pair(NCH // 2 - 1, True)

            @block.tensor
            def _(pe):
                pe.sem_inc(ready, 2)
                pe.wait_ge(w_split, 2)
                with pe.Fori(0, NCH // 2) as cp:
                    for j in range(2):
                        n = 2 * cp + j
                        pe.wait_ge(lo_done, n + 1)
                        pe.wait_ge(added, 2 * cp + 2)
                        for t in range(DT):
                            for dt in range(DT):
                                for p, q in PARTS3:
                                    ins = nc.tensor.matmul(out_ps[j][t][:], w[p][:, dt, t * P:(t + 1) * P], parts[j][q][:, dt, :],
                                                           start=(dt == 0 and (p, q) == (0, 0)),
                                                           stop=(dt == DT - 1 and (p, q) == (1, 0)))
                        ins.then_inc(ready, 1)


def macaron_kernel(nc, xT, w_qT, w_kT, w_vT, w_oT, upT, downT, up_scale, down_scale, output_scale, outT):
    ctx = ExitStack()
    with ctx:
        def sb(n, shape, dt=F32):
            return ctx.enter_context(nc.sbuf_tensor(n, shape, dt))

        def dram(n, shape, dt=F32):
            return nc.dram_tensor(n, shape, dt, kind="Internal").ap()

        x1, x2 = dram("x_after_ffn", [P, DT, TOK]), dram("x_after_attention", [P, DT, TOK])
        qk_parts = [[dram(f"{n}_{part}", [D, TOK]) for part in ("hi", "lo")] for n in ("q", "k")]
        v_scr = dram("v_rows", [TOK, D])
        att = dram("attention_out", [D, TOK])
        sums_scr, inv_scr = dram("prob_sums", [QC, CH]), dram("prob_inverse", [QC, CH])

        ones_mean = sb("ones_mean", [P, P], F32R)
        ones_sum = sb("ones_sum", [P, HD])
        ident = sb("ident", [P, P])
        up_s, down_s, out_s = sb("up_s", [P, HT]), sb("down_s", [P, DT]), sb("out_s", [P, 1])
        vecs = {"up": up_s, "down": down_s}
        const_loaded = ctx.enter_context(nc.semaphore("const_loaded"))
        const_set = ctx.enter_context(nc.semaphore("const_set"))
        scale_set = ctx.enter_context(nc.semaphore("scale_set"))

        with nc.Block() as block:
            @block.sync
            def _(sp):
                sp.dma_start(up_s[:], up_scale).then_inc(const_loaded, 16)
                sp.dma_start(down_s[:], down_scale).then_inc(const_loaded, 16)
                sp.dma_start(out_s[:], output_scale).then_inc(const_loaded, 16)

            @block.gpsimd
            def _(pool):
                nc.gpsimd.memset(f32(ones_mean[:]), 1.0 / D)
                nc.gpsimd.memset(ones_sum[:], 1.0)
                nc.gpsimd.memset(ident[:], 0.0).then_inc(const_set, 1)
                pool.wait_ge(const_set, 1)
                nc.gpsimd.affine_select(out=ident[:], in_=ident[:], compare_op=ALU.not_equal, fill=1.0,
                                        base=0, pattern=[[-1, P]], channel_multiplier=1).then_inc(const_set, 1)

            @block.vector
            def _(dve):
                dve.wait_ge(const_loaded, 48)
                nc.vector.tensor_scalar(down_s[:], down_s[:], out_s[:, 0:1], 0.5, ALU.mult, ALU.mult).then_inc(scale_set, 1)
                dve.wait_ge(scale_set, 1)
                dve.wait_ge(const_set, 2)

        ffn_phase(nc, "ffn1", xT, x1, upT, downT, vecs, ones_mean)
        qkv_phase(nc, x1, (w_qT, w_kT, w_vT), qk_parts, v_scr, ones_mean)
        attention_phase(nc, qk_parts, v_scr, att, sums_scr, inv_scr, ident, ones_sum)
        oproj_phase(nc, att.rearrange("(t p) n -> p t n", p=P), x1, w_oT, x2)
        ffn_phase(nc, "ffn2", x2, outT, upT, downT, vecs, ones_mean)


def kernel(L0_attn_x, L0_attn_w_q, L0_attn_w_k, L0_attn_w_v, L0_attn_w_o, L0_ffn_up_weight, L0_ffn_down_weight,
           L0_ffn_up_scale, L0_ffn_down_scale, L0_ffn_output_scale):
    import numpy as np
    from concourse import bacc
    from concourse.bass_utils import run_bass_kernel_spmd

    def tiles(a):
        a = np.asarray(a)
        return np.ascontiguousarray(a.reshape(-1, P, a.shape[-1]).transpose(1, 0, 2))

    x = np.asarray(L0_attn_x)
    arrays = {
        "xT": tiles(x.reshape(TOK, D).T),
        "w_qT": tiles(np.asarray(L0_attn_w_q).T),
        "w_kT": tiles(np.asarray(L0_attn_w_k).T),
        "w_vT": tiles(np.asarray(L0_attn_w_v).T),
        "w_oT": tiles(np.asarray(L0_attn_w_o).T),
        "upT": tiles(np.asarray(L0_ffn_up_weight).T),
        "downT": tiles(np.asarray(L0_ffn_down_weight).T),
        "up_scale": np.ascontiguousarray(np.asarray(L0_ffn_up_scale).reshape(HT, P).T),
        "down_scale": np.ascontiguousarray(np.asarray(L0_ffn_down_scale).reshape(DT, P).T),
        "output_scale": np.ascontiguousarray(np.broadcast_to(np.asarray(L0_ffn_output_scale).reshape(1, 1), (P, 1))),
    }
    nc = bacc.Bacc("TRN2", target_bir_lowering=False, num_devices=1)
    args = [nc.dram_tensor(n, a.shape, mybir.dt.from_np(a.dtype), kind="ExternalInput").ap() for n, a in arrays.items()]
    out = nc.dram_tensor("outT", (P, DT, TOK), F32, kind="ExternalOutput").ap()
    macaron_kernel(nc, *args, out)
    r = run_bass_kernel_spmd(nc, [arrays], core_ids=[0])
    got = np.asarray(r.results[0]["outT"])
    return np.ascontiguousarray(got.transpose(1, 0, 2).reshape(D, TOK).T).reshape(BATCH, SEQ, D)
```

```python
import concourse.bass as bass
from concourse import mybir
from contextlib import ExitStack

F32 = mybir.dt.float32
F32R = mybir.dt.float32r
ALU = mybir.AluOpType
ACT = mybir.ActivationFunctionType
AX = mybir.AxisListType

P = 128
BATCH, SEQ, D, HID = 2, 2048, 512, 2048
TOK = BATCH * SEQ
HEADS, HD = 16, 32
SCALE = 1.0 / HD ** 0.5
EPS = 1e-5
CH = 512
NCH = TOK // CH
DT = D // P
HT = HID // P
KT = SEQ // P
QC = SEQ // CH
NH = BATCH * HEADS

PARTS3 = ((0, 0), (0, 1), (1, 0))


def f32(ap):
    return ap.bitcast(F32)


NV, NA = 16, 3


class Norm:
    def __init__(self, nc, ctx, tag, ones_mean):
        def sb(n, shape, dt=F32):
            return ctx.enter_context(nc.sbuf_tensor(f"{tag}_{n}", shape, dt))
        self.nc, self.ones = nc, ones_mean
        self.pair = sb("pair", [P, 2, CH])
        self.sum = sb("sum", [P, CH])
        self.sum_hi, self.sum_lo = sb("sum_hi", [P, CH], F32R), sb("sum_lo", [P, CH], F32R)
        self.var, self.std = sb("var", [P, CH]), sb("std", [P, CH])
        self.inv, self.tmp = sb("inv", [P, CH]), sb("tmp", [P, CH])
        self.cent = sb("cent", [P, DT, CH])
        self.work = sb("work", [P, DT, CH])
        self.mean_ps = ctx.enter_context(nc.psum_tensor(f"{tag}_mean", [P, CH], F32))
        self.var_ps = ctx.enter_context(nc.psum_tensor(f"{tag}_varps", [P, CH], F32))
        self.dve = ctx.enter_context(nc.semaphore(f"{tag}_norm_dve"))
        self.act = ctx.enter_context(nc.semaphore(f"{tag}_norm_act"))
        self.pe = ctx.enter_context(nc.semaphore(f"{tag}_norm_pe"))

    def vector(self, dve, k, m, x, lo, hi):
        nc = self.nc
        if k not in (0, 4, 5, 9, 10, 15):
            dve.wait_ge(self.dve, m * NV + k)
        if k == 0:
            ins = nc.vector.tensor_tensor(self.pair[:], x[:, 0:2, :], x[:, 2:4, :], ALU.add)
        elif k == 1:
            ins = nc.vector.tensor_tensor(self.sum[:], self.pair[:, 0, :], self.pair[:, 1, :], ALU.add)
        elif k == 2:
            ins = nc.vector.tensor_copy(self.sum_hi[:], self.sum[:])
        elif k == 3:
            ins = nc.vector.tensor_tensor(self.sum_lo[:], self.sum[:], f32(self.sum_hi[:]), ALU.subtract)
        elif k == 4:
            dve.wait_ge(self.pe, m * 2 + 1)
            mean = self.mean_ps[:].unsqueeze(1).to_broadcast([P, DT, CH])
            ins = nc.vector.tensor_tensor(self.cent[:], x, mean, ALU.subtract)
        elif k == 5:
            dve.wait_ge(self.act, m * NA + 1)
            ins = nc.vector.tensor_tensor(self.pair[:], self.work[:, 0:2, :], self.work[:, 2:4, :], ALU.add)
        elif k == 6:
            ins = nc.vector.tensor_tensor(self.sum[:], self.pair[:, 0, :], self.pair[:, 1, :], ALU.add)
        elif k == 7:
            ins = nc.vector.tensor_copy(self.sum_hi[:], self.sum[:])
        elif k == 8:
            ins = nc.vector.tensor_tensor(self.sum_lo[:], self.sum[:], f32(self.sum_hi[:]), ALU.subtract)
        elif k == 9:
            dve.wait_ge(self.pe, m * 2 + 2)
            ins = nc.vector.tensor_scalar(self.var[:], self.var_ps[:], EPS, None, ALU.add)
        elif k == 10:
            dve.wait_ge(self.act, m * NA + 2)
            ins = nc.vector.reciprocal(self.inv[:], self.std[:])
        elif k == 11:
            ins = nc.vector.scalar_tensor_tensor(self.tmp[:], self.var[:], -0.5, self.inv[:], ALU.mult, ALU.mult)
        elif k == 12:
            ins = nc.vector.tensor_tensor(self.tmp[:], self.tmp[:], self.inv[:], ALU.mult)
        elif k == 13:
            ins = nc.vector.scalar_tensor_tensor(self.inv[:], self.tmp[:], 1.5, self.inv[:], ALU.add, ALU.mult)
        elif k == 14:
            inv = self.inv[:].unsqueeze(1).to_broadcast([P, DT, CH])
            ins = nc.vector.tensor_tensor(self.work[:], self.cent[:], inv, ALU.mult)
        elif k == 15:
            dve.wait_ge(self.act, m * NA + 3)
            ins = nc.vector.tensor_tensor(lo, self.work[:], f32(hi), ALU.subtract)
        ins.then_inc(self.dve, 1)

    def scalar(self, act, k, m, hi):
        nc = self.nc
        act.wait_ge(self.dve, m * NV + (5, 10, 15)[k])
        if k == 0:
            ins = nc.scalar.activation(self.work[:], self.cent[:], ACT.Square)
        elif k == 1:
            ins = nc.scalar.activation(self.std[:], self.var[:], ACT.Sqrt)
        else:
            ins = nc.scalar.activation(hi, self.work[:], ACT.Copy)
        ins.then_inc(self.act, 1)

    def tensor(self, pe, k, m):
        nc = self.nc
        pe.wait_ge(self.dve, m * NV + (4, 9)[k])
        out = (self.mean_ps, self.var_ps)[k]
        nc.tensor.matmul(out[:], self.ones[:], self.sum_hi[:], start=True, stop=False)
        nc.tensor.matmul(out[:], self.ones[:], self.sum_lo[:], start=False, stop=True).then_inc(self.pe, 1)


class Stream:

    def __init__(self, nc, ctx, tag, ones_mean):
        def sb(n, dt=F32):
            return ctx.enter_context(nc.sbuf_tensor(f"{tag}_{n}", [P, DT, CH], dt))
        self.x = [sb(f"x{i}") for i in range(2)]
        self.out = sb("out")
        self.hi = [sb(f"hi{i}", F32R) for i in range(2)]
        self.lo = [sb(f"lo{i}", F32R) for i in range(2)]
        self.norm = Norm(nc, ctx, tag, ones_mean)
        self.loaded = [ctx.enter_context(nc.semaphore(f"{tag}_loaded{i}")) for i in range(2)]
        self.stored = ctx.enter_context(nc.semaphore(f"{tag}_stored"))

    def load(self, sp, j, src, n):
        sp.dma_start(self.x[j][:], chunk(src, n)).then_inc(self.loaded[j], 16)

    def vector_norm(self, dve, k, m, j):
        self.norm.vector(dve, k, m, self.x[j][:], self.lo[j][:], self.hi[j][:])

    def scalar_norm(self, act, k, m, j):
        self.norm.scalar(act, k, m, self.hi[j][:])


class Signs:

    def __init__(self, nc, ctx, tag, up_raw, down_raw, stages):
        self.nc, self.up_raw, self.down_raw, self.stages = nc, up_raw, down_raw, stages
        self.up = ctx.enter_context(nc.sbuf_tensor(f"{tag}_up_w", [P, DT, HID], F32R))
        self.down = ctx.enter_context(nc.sbuf_tensor(f"{tag}_down_w", [P, HT, D], F32R))
        self.loaded = [ctx.enter_context(nc.semaphore(f"{tag}_sign_loaded{i}")) for i in range(2)]
        self.made = ctx.enter_context(nc.semaphore(f"{tag}_sign_made"))

    def stage(self, q):
        return self.stages[q % 2][:].rearrange("p a b -> p (a b)")

    def load(self, sp, q):
        if q >= 2:
            sp.wait_ge(self.made, q - 1)
        src = self.up_raw[:, q, :] if q < 4 else self.down_raw[:, 4 * (q - 4):4 * (q - 3), :].rearrange("p a b -> p (a b)")
        sp.dma_start(self.stage(q), src).then_inc(self.loaded[q % 2], 16)

    def make(self, act, q):
        act.wait_ge(self.loaded[q % 2], 16 * (q // 2 + 1))
        dst = self.up[:, q, :] if q < 4 else self.down[:, 4 * (q - 4):4 * (q - 3), :].rearrange("p a b -> p (a b)")
        self.nc.scalar.activation(dst, self.stage(q), ACT.Sign).then_inc(self.made, 1)


def chunk(ap, n):
    return ap[:, :, bass.ds(n * CH, CH)]


def ffn_phase(nc, tag, st, signs, first_norm, x_in, x_out, next_in, m0, l0, vecs, qkv_stage=None):
    with ExitStack() as ctx:
        def sb(n, shape, dt=F32):
            return ctx.enter_context(nc.sbuf_tensor(f"{tag}_{n}", shape, dt))

        def ps(n):
            return ctx.enter_context(nc.psum_tensor(f"{tag}_{n}", [P, CH], F32))

        def sem(n):
            return ctx.enter_context(nc.semaphore(f"{tag}_{n}"))

        RING, RAW = 4, 2
        hid_hi, hid_lo = sb("hid_hi", [P, RING, CH], F32R), sb("hid_lo", [P, RING, CH], F32R)
        hid = sb("hid", [P, RAW, CH])
        norm, x, parts = st.norm, st.x, (st.hi, st.lo)
        up_ps = [ps(f"up{i}") for i in range(2)]
        down_ps = [ps(f"down{i}") for i in range(DT)]

        up_ready = sem("up_ready")
        up_read = sem("up_read")
        hid_ready = sem("hid_ready")
        hid_used = sem("hid_used")
        down_read = sem("down_read")
        out_stored = sem("out_stored")
        LAG = 3
        DVE_AT = {3: (0, 1), 4: (2, 3), 6: (4,), 8: (5, 6), 9: (7, 8), 11: (9,), 12: (10,),
                  13: (11, 12), 14: (13, 14), 15: (15,)}
        ACT_AT = {6: 0, 11: 1, 14: 2}
        PE_AT = {6: 0, 11: 1}
        NP = NCH // 2

        with nc.Block() as block:
            def pairs(eng, body):
                with eng.Fori(0, NP - 1) as cp:
                    body(cp, False)
                body(NP - 1, True)

            def ahead(last, j):
                return next_in is not None or not (last and j)

            @block.sync
            def _(sp):
                sp.sem_inc(out_stored, 16)
                if first_norm:
                    st.load(sp, 0, x_in, 0)
                    for q in range(8):
                        signs.load(sp, q)
                    sp.wait_ge(signs.made, 8)
                    st.load(sp, 1, x_in, 1)
                    if qkv_stage:
                        for w, raw in enumerate(qkv_stage["raw"]):
                            sp.dma_start(qkv_stage["buf"][:, w], raw).then_inc(qkv_stage["loaded"], 16)
                else:
                    st.load(sp, 1, x_in, 1)

                def pair(cp, last):
                    for j in range(2):
                        n = 2 * cp + j
                        sp.wait_ge(down_read, n + 2)
                        if not last:
                            st.load(sp, j, x_in, n + 2)
                        elif j == 0 and next_in is not None:
                            sp.wait_ge(out_stored, 32)
                            st.load(sp, 0, next_in, 0)
                        sp.dma_start(chunk(x_out, n), st.out[:]).then_inc(out_stored, 16)
                pairs(sp, pair)
                sp.wait_ge(out_stored, 16 * NCH + 16)

            @block.vector
            def _(dve):
                dve.sem_inc(hid_ready, RAW)
                dve.sem_inc(down_read, 1)
                if first_norm:
                    dve.wait_ge(st.loaded[0], 16)
                    for k in range(NV):
                        st.vector_norm(dve, k, m0, 0)

                def pair(cp, last):
                    for j in range(2):
                        n = 2 * cp + j
                        for ht in range(HT):
                            dve.wait_ge(up_read, 2 + n * HT + ht + 1)
                            nc.vector.tensor_tensor(hid_lo[:, ht % RING, :], hid[:, ht % RAW, :],
                                                    f32(hid_hi[:, ht % RING, :]), ALU.subtract).then_inc(hid_ready, 1)
                            if ahead(last, j):
                                if ht == 3:
                                    dve.wait_ge(st.loaded[1 - j], 16 * (cp + j) + 16 + 8 * l0)
                                for k in DVE_AT.get(ht, ()):
                                    st.vector_norm(dve, k, n + 1 + m0, 1 - j)
                        dve.wait_ge(hid_used, RING + n * HT + HT)
                        dve.wait_ge(out_stored, 16 * n + 16)
                        for dt in range(DT):
                            ins = nc.vector.scalar_tensor_tensor(st.out[:, dt, :], down_ps[dt][:], vecs["down"][:, dt:dt + 1],
                                                                 x[j][:, dt, :], ALU.mult, ALU.add)
                        ins.then_inc(down_read, 1)
                pairs(dve, pair)

            @block.scalar
            def _(act):
                act.sem_inc(up_read, 2)
                if first_norm:
                    for q in range(2):
                        signs.make(act, q)
                    st.scalar_norm(act, 0, m0, 0)
                    for q in range(2, 4):
                        signs.make(act, q)
                    st.scalar_norm(act, 1, m0, 0)
                    for q in range(4, 6):
                        signs.make(act, q)
                    st.scalar_norm(act, 2, m0, 0)
                    for q in range(6, 8):
                        signs.make(act, q)

                def pair(cp, last):
                    for j in range(2):
                        n = 2 * cp + j
                        for ht in range(HT):
                            act.wait_ge(up_ready, n * HT + ht + 1)
                            act.wait_ge(hid_ready, n * HT + ht + 1)
                            nc.scalar.activation(hid[:, ht % RAW, :], up_ps[ht % 2][:], ACT.Relu,
                                                 scale=vecs["up"][:, ht:ht + 1])
                            act.wait_ge(hid_used, n * HT + ht + 1)
                            nc.scalar.activation(hid_hi[:, ht % RING, :], up_ps[ht % 2][:], ACT.Relu,
                                                 scale=vecs["up"][:, ht:ht + 1]).then_inc(up_read, 1)
                            if ht in ACT_AT and ahead(last, j):
                                st.scalar_norm(act, ACT_AT[ht], n + 1 + m0, 1 - j)
                pairs(act, pair)

            @block.tensor
            def _(pe):
                pe.sem_inc(hid_used, RING)
                if first_norm:
                    norm.tensor(pe, 0, m0)
                    norm.tensor(pe, 1, m0)
                pe.wait_ge(signs.made, 4)

                def pair(cp, last):
                    for j in range(2):
                        n = 2 * cp + j
                        pe.wait_ge(norm.dve, NV * (n + 1 + m0))
                        for ht in range(HT + LAG):
                            if ht < HT:
                                pe.wait_ge(up_read, n * HT + ht + 1)
                                for dt in range(DT):
                                    for i, part in enumerate(parts):
                                        ins = nc.tensor.matmul(up_ps[ht % 2][:], signs.up[:, dt, ht * P:(ht + 1) * P],
                                                               part[j][:, dt, :], start=(dt == 0 and i == 0),
                                                               stop=(dt == DT - 1 and i == 1))
                                ins.then_inc(up_ready, 1)
                            if ht in PE_AT and ahead(last, j):
                                norm.tensor(pe, PE_AT[ht], n + 1 + m0)
                            h = ht - LAG
                            if h >= 0:
                                if h == 0:
                                    pe.wait_ge(down_read, n + 1)
                                if h % 4 == 0 and first_norm:
                                    pe.wait_ge(signs.made, 5 + h // 4)
                                pe.wait_ge(hid_ready, RAW + n * HT + h + 1)
                                for dt in range(DT):
                                    for i, part in enumerate((hid_hi, hid_lo)):
                                        ins = nc.tensor.matmul(down_ps[dt][:], signs.down[:, h, dt * P:(dt + 1) * P],
                                                               part[:, h % RING, :], start=(h == 0 and i == 0),
                                                               stop=(h == HT - 1 and i == 1))
                                ins.then_inc(hid_used, 1)
                pairs(pe, pair)


def qkv_phase(nc, st, x_in, m0, l0, w_st, w_loaded, qk_parts, v_scr):
    with ExitStack() as ctx:
        def sb(n, shape, dt=F32):
            return ctx.enter_context(nc.sbuf_tensor(f"qkv_{n}", shape, dt))

        def sem(n):
            return ctx.enter_context(nc.semaphore(f"qkv_{n}"))

        w_hi, w_lo = sb("w_hi", [P, 3, DT, D], F32R), sb("w_lo", [P, 3, DT, D], F32R)
        norm, xh, xl = st.norm, st.hi, st.lo
        RING = 4
        o_hi, o_lo = sb("o_hi", [P, RING, CH], F32R), sb("o_lo", [P, RING, CH], F32R)
        o_v = sb("o_v", [P, RING, CH])
        out_ps = [ctx.enter_context(nc.psum_tensor(f"qkv_o{i}", [P, CH], F32)) for i in range(RING)]
        w_rounded, w_split = sem("w_rounded"), sem("w_split")
        out_ready = sem("out_ready")
        act_read = sem("act_read")
        out_read = sem("out_read")
        stored = [sem(f"stored{i}") for i in range(RING)]
        NT = 12
        PER = 80
        BEFORE = (16, 48, 80)

        with nc.Block() as block:
            @block.sync
            def _(sp):
                for s in range(RING):
                    sp.sem_inc(stored[s], 16)
                st.load(sp, 1, x_in, 1)

                def pair(cp, last):
                    for j in range(2):
                        n = 2 * cp + j
                        if not last:
                            sp.wait_ge(norm.dve, NV * (n + 1 + m0))
                            st.load(sp, j, x_in, n + 2)
                        for t in range(NT):
                            sp.wait_ge(out_read, RING + n * NT + t + 1)
                            s = t % RING
                            if t < 8:
                                rows = slice((t % 4) * P, (t % 4 + 1) * P)
                                for part, src in ((0, o_hi), (1, o_lo)):
                                    dst = qk_parts[t // 4][part][rows, bass.ds(n * CH, CH)]
                                    sp.dma_start(dst, f32(src[:, s, :])).then_inc(stored[s], 16)
                            else:
                                sp.dma_start(v_scr[bass.ds(n * CH + (t - 8) * P, P), :], o_v[:, s, :]).then_inc(stored[s], 16)
                with sp.Fori(0, NCH // 2 - 1) as cp:
                    pair(cp, False)
                pair(NCH // 2 - 1, True)
                for s in range(RING):
                    sp.wait_ge(stored[s], PER * NCH + 16)

            DVE_AT = {-1: (0, 1, 2, 3), 1: (4,), 2: (5, 6, 7, 8), 4: (9,), 5: (10, 11, 12, 13, 14), 8: (15,)}
            ACT_AT = {1: 0, 4: 1, 7: 2}
            PE_AT = {1: 0, 4: 1}

            @block.vector
            def _(dve):
                dve.sem_inc(out_read, RING)
                for w in range(3):
                    dve.wait_ge(w_rounded, w + 1)
                    nc.vector.tensor_tensor(w_lo[:, w], w_st[:, w], f32(w_hi[:, w]), ALU.subtract).then_inc(w_split, 1)

                def pair(cp, last):
                    for j in range(2):
                        n = 2 * cp + j
                        if not (last and j):
                            dve.wait_ge(st.loaded[1 - j], 16 * (cp + j) + 16 + 8 * l0)
                            for k in DVE_AT[-1]:
                                st.vector_norm(dve, k, n + 1 + m0, 1 - j)
                        for t in range(NT):
                            s = t % RING
                            if t < 8:
                                dve.wait_ge(act_read, n * 8 + t + 1)
                                nc.vector.tensor_tensor(o_lo[:, s, :], out_ps[s][:], f32(o_hi[:, s, :]),
                                                        ALU.subtract).then_inc(out_read, 1)
                            else:
                                dve.wait_ge(stored[s], n * PER + BEFORE[2])
                                dve.wait_ge(out_ready, n * NT + t + 1)
                                nc.vector.tensor_copy(o_v[:, s, :], out_ps[s][:]).then_inc(out_read, 1)
                            if not (last and j):
                                for k in DVE_AT.get(t, ()):
                                    st.vector_norm(dve, k, n + 1 + m0, 1 - j)
                with dve.Fori(0, NCH // 2 - 1) as cp:
                    pair(cp, False)
                pair(NCH // 2 - 1, True)

            @block.scalar
            def _(act):
                act.wait_ge(w_loaded, 48)
                for w in range(3):
                    nc.scalar.activation(w_hi[:, w], w_st[:, w], ACT.Copy).then_inc(w_rounded, 1)

                def pair(cp, last):
                    for j in range(2):
                        n = 2 * cp + j
                        for t in range(NT):
                            s = t % RING
                            if t < 8:
                                act.wait_ge(stored[s], n * PER + BEFORE[t // 4])
                                act.wait_ge(out_ready, n * NT + t + 1)
                                nc.scalar.activation(o_hi[:, s, :], out_ps[s][:], ACT.Copy).then_inc(act_read, 1)
                            if t in ACT_AT and not (last and j):
                                st.scalar_norm(act, ACT_AT[t], n + 1 + m0, 1 - j)
                with act.Fori(0, NCH // 2 - 1) as cp:
                    pair(cp, False)
                pair(NCH // 2 - 1, True)

            @block.tensor
            def _(pe):
                w = (w_hi, w_lo)

                def pair(cp, last):
                    for j in range(2):
                        n = 2 * cp + j
                        act_parts = (xh[j], xl[j])
                        pe.wait_ge(norm.dve, NV * (n + 1 + m0))
                        for t in range(NT):
                            which, i = t // 4, t % 4
                            if i == 0:
                                pe.wait_ge(w_split, which + 1)
                            pe.wait_ge(out_read, n * NT + t + 1)
                            for dt in range(DT):
                                for a, b in PARTS3:
                                    if which < 2:
                                        left, right = w[a][:, which, dt, i * P:(i + 1) * P], act_parts[b][:, dt, :]
                                    else:
                                        left, right = act_parts[b][:, dt, i * P:(i + 1) * P], w[a][:, which, dt, :]
                                    ins = nc.tensor.matmul(out_ps[t % RING][:], left, right,
                                                           start=(dt == 0 and (a, b) == (0, 0)),
                                                           stop=(dt == DT - 1 and (a, b) == (1, 0)))
                            ins.then_inc(out_ready, 1)
                            if t in PE_AT and not (last and j):
                                norm.tensor(pe, PE_AT[t], n + 1 + m0)
                with pe.Fori(0, NCH // 2 - 1) as cp:
                    pair(cp, False)
                pair(NCH // 2 - 1, True)


def bank_order(units, banks, second):
    ages, bank = list(range(banks)), []
    for i in range(units):
        b = ages.pop(1 if i in second else 0)
        ages.append(b)
        bank.append(b)
    assert ages == list(range(banks))
    last = {b: u - units for u, b in enumerate(bank)}
    freed = []
    for i, b in enumerate(bank):
        freed.append(last[b] + 1)
        last[b] = i
    return bank, freed


def attention_phase(nc, qk_parts, v_scr, att, sums_scr, inv_scr, ident, ones_sum, wo_raw, wo):
    NB = 4
    KQ, KM = 3 * HD, 3 * HD + 2
    LEAD, LAG = 4, 2
    PR = 8
    SR, MR = 3, 3
    UNITS = KT * QC
    S_BANK, S_FREED = bank_order(UNITS, SR, (23, 46))
    M_BANK, M_FREED = bank_order(UNITS, MR, (22, 51))
    POOLED = (0, 1, 2, 4, 5, 7, 8, 10, 11, 13, 14)
    UNPOOLED = 3
    NA_ = len(POOLED) - 1
    PER = 7 * 16
    with ExitStack() as ctx:
        def sb(n, shape, dt=F32):
            return ctx.enter_context(nc.sbuf_tensor(f"att_{n}", shape, dt))

        def ps(n):
            return ctx.enter_context(nc.psum_tensor(f"att_{n}", [P, CH], F32))

        def sem(n):
            return ctx.enter_context(nc.semaphore(f"att_{n}"))

        q_st = [sb(f"q{i}", [P, SEQ], F32R) for i in range(NB)]
        k_st = [sb(f"k{i}", [P, SEQ], F32R) for i in range(NB)]
        v_st = [sb(f"v{i}", [P, KT, HD]) for i in range(NB)]
        prob = [sb(f"p{i}", [P, SEQ]) for i in range(PR)]
        acc = [sb(f"acc{i}", [P, SEQ]) for i in range(2)]
        row_max = [sb(f"row_max{i}", [P, KT, QC]) for i in range(2)]
        neg_max = sb("neg_max", [P, KT])
        neg_parts = sb("neg_parts", [P, 2, KT], F32R)
        neg_rows = sb("neg_rows", [2 * KT, P], F32R)
        un, total = sb("un", [P, CH]), sb("total", [P, CH])
        tot_t, inv_t = sb("tot_t", [P, KT]), sb("inv_t", [P, KT])
        inv_b, fin = sb("inv_b", [P, CH]), sb("fin", [P, CH])
        s_ps = [ps(f"s{i}") for i in range(SR)]
        m_ps = [ps(f"m{i}") for i in range(MR)]
        o_ps, t_ps = ps("o"), ps("t")

        loaded = [sem(f"loaded{i}") for i in range(NB)]
        ones_set = sem("ones_set")
        m_ready, m_read = sem("m_ready"), sem("m_read")
        neg_dve, neg_pe = sem("neg_dve"), sem("neg_pe")
        neg_loaded = sem("neg_loaded")
        s_ready, exp_done = sem("s_ready"), sem("exp_done")
        p_used = sem("p_used")
        summed = sem("summed")
        t_ready, evac = sem("t_ready"), sem("evac")
        tail = sem("tail")
        TURN = KT - LEAD + 1
        t_bank = m_ps[M_BANK[QC + 2]]
        wo_loaded, wo_done = sem("wo_loaded"), sem("wo_done")
        div = sem("div")

        def adds_before(kt):
            return max(1, POOLED.index(kt))

        with nc.Block() as block:
            def groups(eng, body):
                body(0, True, False)
                with eng.Fori(1, NH // NB - 1) as g:
                    body(g, False, False)
                body(NH // NB - 1, False, True)

            @block.sync
            def _(sp):
                def load(b, row, col):
                    for which, st in ((0, q_st[b]), (1, k_st[b])):
                        for i, part in enumerate(((0, 0, 1), (0, 1, 0))[which]):
                            sp.dma_start(f32(st[i * HD:(i + 1) * HD, :]),
                                         qk_parts[which][part][bass.ds(row, HD), bass.ds(col, SEQ)]).then_inc(loaded[b], 16)
                    sp.dma_start(v_st[b][:], v_scr[bass.ds(col, SEQ), bass.ds(row, HD)].rearrange("(t p) d -> p t d", p=P)
                                 ).then_inc(loaded[b], 16)

                def max_rows(b, H):
                    sp.wait_ge(neg_dve, 4 * H + 4)
                    for r in range(2):
                        sp.dma_start(f32(q_st[b][KQ + r:KQ + r + 1, :].rearrange("o (t p) -> o t p", p=P)),
                                     f32(neg_rows[r * KT:(r + 1) * KT, :])).then_inc(neg_loaded, 16)

                def normalise(H, row, col):
                    T = 11 * 16
                    sp.wait_ge(evac, 2 * H + 2)
                    sp.dma_start(sums_scr[:, :], total[0:P:HD, :]).then_inc(tail, 16)
                    sp.wait_ge(tail, T * H + 16)
                    sp.dma_start(tot_t[:], sums_scr.rearrange("a (b c) -> (a b) c", c=KT)).then_inc(tail, 16)
                    sp.wait_ge(div, 2 * H + 1)
                    sp.dma_start(inv_scr.rearrange("a (b c) -> (a b) c", c=KT), inv_t[:]).then_inc(tail, 16)
                    sp.wait_ge(tail, T * H + 48)
                    for c in range(QC):
                        sp.dma_start(inv_b[c * HD:(c + 1) * HD, :], inv_scr[c:c + 1, :].to_broadcast([HD, CH])).then_inc(tail, 16)
                    sp.wait_ge(div, 2 * H + 2)
                    for c in range(QC):
                        sp.dma_start(att[bass.ds(row, HD), bass.ds(col + c * CH, CH)], fin[c * HD:(c + 1) * HD, :]).then_inc(tail, 16)

                for b in range(3):
                    load(b, b * HD, 0)
                sp.dma_start(prob[PR - 1][:], wo_raw.rearrange("p a b -> p (a b)")).then_inc(wo_loaded, 16)
                max_rows(0, 0)

                def body(g, first, last):
                    for j in range(NB):
                        H = NB * g + j
                        if not (last and j):
                            sp.wait_ge(s_ready, 64 * H)
                            sp.wait_ge(p_used, PR + KT * H)
                            X = H + 3
                            load((j + 3) % NB, X % HEADS * HD, X // HEADS * SEQ)
                        if not (first and j == 0):
                            Y = H - 1
                            normalise(Y, Y % HEADS * HD, Y // HEADS * SEQ)
                        if not (last and j == NB - 1):
                            max_rows((j + 1) % NB, H + 1)
                groups(sp, body)
                normalise(NH - 1, (HEADS - 1) * HD, SEQ)
                sp.wait_ge(tail, 11 * 16 * NH)

            @block.gpsimd
            def _(pool):
                for b in range(NB):
                    nc.gpsimd.memset(f32(k_st[b][KQ:KM, :]), 1.0).then_inc(ones_set, 1)
                pool.sem_inc(summed, NA_)
                pool.wait_ge(ones_set, NB)
                pool.wait_ge(wo_done, 1)
                nc.gpsimd.tensor_tensor(wo[1][:].rearrange("p a b -> p (a b)"), prob[PR - 1][:],
                                        f32(wo[0][:].rearrange("p a b -> p (a b)")), ALU.subtract).then_inc(wo_done, 1)

                def body(g, first, last):
                    for j in range(NB):
                        H = NB * g + j
                        for i, kt in enumerate(POOLED):
                            if i == 0:
                                continue
                            pool.wait_ge(exp_done, SR + 64 * H + 4 * kt + 4)
                            if i == 1:
                                if not (first and j < 2):
                                    pool.wait_ge(t_ready, H - 1)
                                a = prob[POOLED[0] % PR]
                            else:
                                pool.wait_ge(summed, NA_ * (H + 1) + i - 1)
                                a = acc[j % 2]
                            nc.gpsimd.tensor_tensor(acc[j % 2][:], a[:], prob[kt % PR][:], ALU.add).then_inc(summed, 1)
                groups(pool, body)

            @block.vector
            def _(dve):
                dve.sem_inc(m_read, MR)

                def reduce_tile(T, odd, qt, chunks=range(QC)):
                    for c in chunks:
                        dve.wait_ge(m_ready, QC * T + c + 1)
                        nc.vector.tensor_reduce(row_max[odd][:, qt, c:c + 1], m_ps[M_BANK[qt * QC + c]][:], axis=AX.X, op=ALU.max).then_inc(m_read, 1)

                def negate(step, T_end, odd, h):
                    if step == 0:
                        dve.wait_ge(m_read, MR + QC * T_end)
                        nc.vector.tensor_reduce(neg_max[:], row_max[odd][:], axis=AX.X, op=ALU.max, negate=True).then_inc(neg_dve, 1)
                        return
                    dve.wait_ge(neg_dve, 4 * h + step)
                    if step == 1:
                        nc.vector.tensor_copy(neg_parts[:, 0, :], neg_max[:]).then_inc(neg_dve, 1)
                    else:
                        nc.vector.tensor_tensor(neg_parts[:, 1, :], neg_max[:], f32(neg_parts[:, 0, :]), ALU.subtract).then_inc(neg_dve, 1)

                def rows_out(h, wait):
                    dve.wait_ge(neg_pe, h + 1)
                    if wait:
                        dve.wait_ge(neg_loaded, 32 * h)
                    nc.vector.tensor_copy(neg_rows[:], t_bank[0:2 * KT, 0:P]).then_inc(neg_dve, 1)

                T = 0
                for qt in range(KT):
                    reduce_tile(qt, 0, qt)
                for step in range(3):
                    negate(step, KT, 0, 0)
                rows_out(0, False)
                for qt in range(LEAD):
                    reduce_tile(KT + qt, 1, qt)

                def body(g, first, last):
                    for j in range(NB):
                        H = NB * g + j
                        for kt in range(KT):
                            step_max = not (last and (j == NB - 1 or (j == NB - 2 and kt + LEAD >= KT)))
                            qt = (kt + LEAD) % KT
                            odd = (j + 1 + (kt + LEAD) // KT) % 2
                            if kt == TURN:
                                if step_max:
                                    reduce_tile(KT * (H + 1) + kt + LEAD, odd, qt, (0, 1))
                                if not (last and j == NB - 1):
                                    rows_out(H + 1, True)
                                if step_max:
                                    reduce_tile(KT * (H + 1) + kt + LEAD, odd, qt, (2, 3))
                            elif kt == TURN - 1 and not (last and j == NB - 1):
                                negate(0, KT * (H + 2), (j + 1) % 2, H + 1)
                                for c in range(QC):
                                    if step_max:
                                        reduce_tile(KT * (H + 1) + kt + LEAD, odd, qt, (c,))
                                    if c < 2:
                                        negate(c + 1, KT * (H + 2), (j + 1) % 2, H + 1)
                            elif step_max:
                                reduce_tile(KT * (H + 1) + kt + LEAD, odd, qt)
                            if not (first and j == 0):
                                if kt == 7:
                                    dve.wait_ge(tail, 176 * (H - 1) + 32)
                                    nc.vector.reciprocal(inv_t[:], tot_t[:]).then_inc(div, 1)
                                if kt == 10:
                                    dve.wait_ge(tail, 176 * (H - 1) + 112)
                                    nc.vector.tensor_tensor(fin[:], un[:], inv_b[:], ALU.mult).then_inc(div, 1)
                groups(dve, body)
                dve.wait_ge(tail, 176 * (NH - 1) + 32)
                nc.vector.reciprocal(inv_t[:], tot_t[:]).then_inc(div, 1)
                dve.wait_ge(tail, 176 * (NH - 1) + 112)
                nc.vector.tensor_tensor(fin[:], un[:], inv_b[:], ALU.mult).then_inc(div, 1)

            @block.scalar
            def _(act):
                act.sem_inc(exp_done, SR)
                act.wait_ge(wo_loaded, 16)
                nc.scalar.activation(wo[0][:].rearrange("p a b -> p (a b)"), prob[PR - 1][:], ACT.Copy).then_inc(wo_done, 1)
                act.wait_ge(wo_done, 2)

                def copy_out(H):
                    act.wait_ge(p_used, PR + KT * H + KT)
                    if not isinstance(H, int) or H > 0:
                        act.wait_ge(div, 2 * H)
                    nc.scalar.activation(un[:], o_ps[:], ACT.Copy).then_inc(evac, 1)

                def copy_sums(H):
                    act.wait_ge(t_ready, H + 1)
                    if not isinstance(H, int) or H > 0:
                        act.wait_ge(tail, 176 * (H - 1) + 32)
                    nc.scalar.activation(total[:], t_ps[:], ACT.Copy).then_inc(evac, 1)

                def body(g, first, last):
                    for j in range(NB):
                        H = NB * g + j
                        for kt in range(KT):
                            if not (first and j == 0):
                                if kt == LAG:
                                    copy_out(H - 1)
                                if kt == LAG + 2:
                                    copy_sums(H - 1)
                            act.wait_ge(p_used, KT * H + kt + 1)
                            old = (kt - PR) % KT
                            if old in POOLED:
                                h_old = H if kt >= PR else H - 1
                                act.wait_ge(summed, NA_ * (h_old + 1) + adds_before(old))
                            for c in range(QC):
                                act.wait_ge(s_ready, 64 * H + 4 * kt + c + 1)
                                nc.scalar.activation(prob[kt % PR][:, c * CH:(c + 1) * CH], s_ps[S_BANK[kt * QC + c]][:], ACT.Exp,
                                                     scale=SCALE).then_inc(exp_done, 1)
                groups(act, body)
                copy_out(NH - 1)
                copy_sums(NH - 1)

            @block.tensor
            def _(pe):
                pe.sem_inc(p_used, PR)
                pe.wait_ge(ones_set, NB)

                def maxima(b, T, qt, c):
                    i = qt * QC + c
                    pe.wait_ge(m_read, MR + QC * (T - qt) + M_FREED[i])
                    nc.tensor.matmul(m_ps[M_BANK[i]][:], q_st[b][0:KQ, qt * P:(qt + 1) * P], k_st[b][0:KQ, c * CH:(c + 1) * CH],
                                     start=True, stop=True).then_inc(m_ready, 1)

                def transpose_max(h):
                    pe.wait_ge(neg_dve, 4 * h + 3)
                    nc.tensor.transpose(t_bank[0:2 * KT, 0:P], f32(neg_parts[:].rearrange("p a b -> p (a b)")),
                                        ident[:]).then_inc(neg_pe, 1)

                def out_tile(H, b, kt):
                    pe.wait_ge(exp_done, SR + 64 * H + 4 * kt + 4)
                    if kt == 0 and not (isinstance(H, int) and H == 0):
                        pe.wait_ge(evac, 2 * H - 1)
                    for c in range(QC):
                        rows = slice(c * HD, (c + 1) * HD)
                        ins = nc.tensor.matmul(o_ps[rows, :], v_st[b][:, kt, :], prob[kt % PR][:, c * CH:(c + 1) * CH],
                                               start=(kt == 0), stop=(kt == KT - 1))
                    if kt not in POOLED:
                        if kt == UNPOOLED and not (isinstance(H, int) and H == 0):
                            pe.wait_ge(evac, 2 * H)
                        for c in range(QC):
                            rows = slice(c * HD, (c + 1) * HD)
                            ins = nc.tensor.matmul(t_ps[rows, :], ones_sum[:], prob[kt % PR][:, c * CH:(c + 1) * CH],
                                                   start=(kt == UNPOOLED), stop=False)
                    ins.then_inc(p_used, 1)

                def pooled_sums(H, b2):
                    pe.wait_ge(summed, NA_ * (H + 2))
                    for c in range(QC):
                        rows = slice(c * HD, (c + 1) * HD)
                        ins = nc.tensor.matmul(t_ps[rows, :], ones_sum[:], acc[b2][:, c * CH:(c + 1) * CH],
                                               start=False, stop=True)
                    ins.then_inc(t_ready, 1)

                pe.wait_ge(loaded[0], PER)
                for qt in range(KT):
                    for c in range(QC):
                        maxima(0, qt, qt, c)
                transpose_max(0)
                pe.wait_ge(loaded[1], PER)
                pe.wait_ge(neg_dve, 4)
                for qt in range(LEAD):
                    for c in range(QC):
                        maxima(1, KT + qt, qt, c)

                def body(g, first, last):
                    for j in range(NB):
                        H = NB * g + j
                        pe.wait_ge(neg_loaded, 32 * (H + 1))
                        for kt in range(KT):
                            step_max = not (last and (j == NB - 1 or (j == NB - 2 and kt + LEAD >= KT)))
                            b, qt = ((j + 1) % NB, kt + LEAD) if kt + LEAD < KT else ((j + 2) % NB, kt + LEAD - KT)
                            T = KT * (H + 1) + kt + LEAD
                            def scores(c):
                                i = kt * QC + c
                                pe.wait_ge(exp_done, SR + UNITS * H + S_FREED[i])
                                nc.tensor.matmul(s_ps[S_BANK[i]][:], k_st[j][0:KM, kt * P:(kt + 1) * P],
                                                 q_st[j][0:KM, c * CH:(c + 1) * CH], start=True, stop=True).then_inc(s_ready, 1)

                            if step_max and kt == KT - LEAD:
                                pe.wait_ge(loaded[b], PER * (g + 1 + (j + 2) // NB))
                            for c in (0, 1):
                                scores(c)
                                if step_max:
                                    maxima(b, T, qt, c)
                            if kt == TURN and not (last and j == NB - 1):
                                if step_max:
                                    pe.wait_ge(m_read, MR + UNITS * (H + 2) + M_FREED[QC + 2])
                                transpose_max(H + 1)
                            if kt >= LAG:
                                out_tile(H, j, kt - LAG)
                            elif not (first and j == 0):
                                out_tile(H - 1, (j - 1) % NB, KT + kt - LAG)
                            if kt == LAG + 1 and not (first and j == 0):
                                pooled_sums(H - 1, (j - 1) % 2)
                            for c in (2, 3):
                                scores(c)
                                if step_max:
                                    if kt == TURN and c == 2:
                                        pe.wait_ge(neg_dve, 4 * (H + 1) + 4)
                                    maxima(b, T, qt, c)
                groups(pe, body)
                for kt in range(KT - LAG, KT):
                    out_tile(NH - 1, NB - 1, kt)
                pooled_sums(NH - 1, (NH - 1) % 2)


def oproj_phase(nc, st, signs, att, x_in, wo, x_out):
    with ExitStack() as ctx:
        def sem(n):
            return ctx.enter_context(nc.semaphore(f"op_{n}"))

        a = [ctx.enter_context(nc.sbuf_tensor(f"op_a{i}", [P, DT, CH], F32)) for i in range(2)]
        parts = [(st.hi[i], st.lo[i]) for i in range(2)]
        out_ps = [ctx.enter_context(nc.psum_tensor(f"op_o{i}", [P, CH], F32)) for i in range(DT)]
        a_loaded = [sem(f"a_loaded{i}") for i in range(2)]
        hi_done, lo_done = sem("hi_done"), sem("lo_done")
        ready = sem("ready")
        added = sem("added")
        out_stored = sem("out_stored")

        with nc.Block() as block:
            NP = NCH // 2

            def pairs(eng, body):
                with eng.Fori(0, NP - 1) as cp:
                    body(cp, False)
                body(NP - 1, True)

            @block.sync
            def _(sp):
                sp.sem_inc(out_stored, 16)

                def load_a(j, n):
                    sp.dma_start(a[j][:], chunk(att, n)).then_inc(a_loaded[j], 16)
                for j in range(2):
                    load_a(j, j)
                    st.load(sp, j, x_in, j)
                for q in range(2):
                    signs.load(sp, q)

                def pair(cp, last):
                    for j in range(2):
                        n = 2 * cp + j
                        sp.wait_ge(lo_done, n + 1)
                        if not last:
                            load_a(j, n + 2)
                        sp.wait_ge(added, DT * (n + 2))
                        if not last:
                            st.load(sp, j, x_in, n + 2)
                        elif j == 0:
                            sp.wait_ge(out_stored, 32)
                            st.load(sp, 0, x_out, 0)
                        sp.dma_start(chunk(x_out, n), st.out[:]).then_inc(out_stored, 16)
                for cp in range(NP):
                    pair(cp, cp == NP - 1)
                    if cp < NP - 1:
                        for q in (2 * cp + 2, 2 * cp + 3):
                            signs.load(sp, q)
                sp.wait_ge(out_stored, 16 * NCH + 16)

            @block.scalar
            def _(act):
                for cp in range(NP):
                    for j in range(2):
                        n = 2 * cp + j
                        act.wait_ge(a_loaded[j], 16 * cp + 16)
                        act.wait_ge(ready, DT * n + DT)
                        nc.scalar.activation(parts[j][0][:], a[j][:], ACT.Copy).then_inc(hi_done, 1)
                        if not (cp == 0 and j == 0):
                            signs.make(act, n - 1)
                signs.make(act, 7)
                for k in range(NA):
                    st.scalar_norm(act, k, 0, 0)

            @block.vector
            def _(dve):
                dve.sem_inc(added, DT)

                def split(j, n):
                    dve.wait_ge(hi_done, n + 1)
                    nc.vector.tensor_tensor(parts[j][1][:], a[j][:], f32(parts[j][0][:]), ALU.subtract).then_inc(lo_done, 1)

                def pair(cp, last):
                    for j in range(2):
                        n = 2 * cp + j
                        if not (last and j):
                            split(1 - j, n + 1)
                        dve.wait_ge(st.loaded[j], 16 * cp + 16)
                        dve.wait_ge(out_stored, 16 * n + 16)
                        for t in range(DT):
                            dve.wait_ge(ready, DT * (n + 2) + t + 1)
                            nc.vector.tensor_tensor(st.out[:, t, :], out_ps[t][:], st.x[j][:, t, :], ALU.add).then_inc(added, 1)
                split(0, 0)
                pairs(dve, pair)
                dve.wait_ge(signs.made, 8)
                dve.wait_ge(st.loaded[0], 16 * NP + 16)
                for k in range(NV):
                    st.vector_norm(dve, k, 0, 0)

            @block.tensor
            def _(pe):
                pe.sem_inc(ready, 2 * DT)
                with pe.Fori(0, NP) as cp:
                    for j in range(2):
                        n = 2 * cp + j
                        pe.wait_ge(lo_done, n + 1)
                        for t in range(DT):
                            pe.wait_ge(added, DT * n + t + 1)
                            for dt in range(DT):
                                for p, q in PARTS3:
                                    ins = nc.tensor.matmul(out_ps[t][:], wo[p][:, dt, t * P:(t + 1) * P], parts[j][q][:, dt, :],
                                                           start=(dt == 0 and (p, q) == (0, 0)),
                                                           stop=(dt == DT - 1 and (p, q) == (1, 0)))
                            ins.then_inc(ready, 1)
                st.norm.tensor(pe, 0, 0)
                st.norm.tensor(pe, 1, 0)


def macaron_kernel(nc, xT, w_qT, w_kT, w_vT, w_oT, upT, downT, up_scale, down_scale, output_scale, outT):
    ctx = ExitStack()
    with ctx:
        def sb(n, shape, dt=F32):
            return ctx.enter_context(nc.sbuf_tensor(n, shape, dt))

        def dram(n, shape, dt=F32):
            return nc.dram_tensor(n, shape, dt, kind="Internal").ap()

        x1, x2 = dram("x_after_ffn", [P, DT, TOK]), dram("x_after_attention", [P, DT, TOK])
        qk_parts = [[dram(f"{n}_{part}", [D, TOK]) for part in ("hi", "lo")] for n in ("q", "k")]
        v_scr = dram("v_rows", [TOK, D])
        att = dram("attention_out", [D, TOK])
        sums_scr, inv_scr = dram("prob_sums", [QC, CH]), dram("prob_inverse", [QC, CH])

        ones_mean = sb("ones_mean", [P, P], F32R)
        ones_sum = sb("ones_sum", [P, HD])
        ident = sb("ident", [P, P])
        up_s, down_s, out_s = sb("up_s", [P, HT]), sb("down_s", [P, DT]), sb("out_s", [P, 1])
        vecs = {"up": up_s, "down": down_s}
        const_loaded = ctx.enter_context(nc.semaphore("const_loaded"))
        const_set = ctx.enter_context(nc.semaphore("const_set"))
        scale_set = ctx.enter_context(nc.semaphore("scale_set"))

        with nc.Block() as block:
            @block.sync
            def _(sp):
                sp.dma_start(up_s[:], up_scale).then_inc(const_loaded, 16)
                sp.dma_start(down_s[:], down_scale).then_inc(const_loaded, 16)
                sp.dma_start(out_s[:], output_scale).then_inc(const_loaded, 16)

            @block.gpsimd
            def _(pool):
                nc.gpsimd.memset(f32(ones_mean[:]), 1.0 / D)
                nc.gpsimd.memset(ones_sum[:], 1.0)
                nc.gpsimd.memset(ident[:], 0.0).then_inc(const_set, 1)
                pool.wait_ge(const_set, 1)
                nc.gpsimd.affine_select(out=ident[:], in_=ident[:], compare_op=ALU.not_equal, fill=1.0,
                                        base=0, pattern=[[-1, P]], channel_multiplier=1).then_inc(const_set, 1)

            @block.vector
            def _(dve):
                dve.wait_ge(const_loaded, 48)
                nc.vector.tensor_scalar(down_s[:], down_s[:], out_s[:, 0:1], 0.5, ALU.mult, ALU.mult).then_inc(scale_set, 1)
                dve.wait_ge(scale_set, 1)
                dve.wait_ge(const_set, 2)

        with ExitStack() as span:
            st = Stream(nc, span, "s1", ones_mean)
            w_st = span.enter_context(nc.sbuf_tensor("qkv_raw", [P, 3, DT, D], F32))
            w_loaded = span.enter_context(nc.semaphore("qkv_raw_loaded"))
            with ExitStack() as part:
                signs = Signs(nc, part, "ffn1", upT, downT, (st.out, st.x[1]))
                ffn_phase(nc, "ffn1", st, signs, True, xT, x1, x1, 0, 0, vecs,
                          {"raw": (w_qT, w_kT, w_vT), "buf": w_st, "loaded": w_loaded})
            qkv_phase(nc, st, x1, NCH, NCH, w_st, w_loaded, qk_parts, v_scr)
        with ExitStack() as span:
            wo = [span.enter_context(nc.sbuf_tensor(f"wo_{part}", [P, DT, D], F32R)) for part in ("hi", "lo")]
            attention_phase(nc, qk_parts, v_scr, att, sums_scr, inv_scr, ident, ones_sum, w_oT, wo)
            st = Stream(nc, span, "s2", ones_mean)
            signs = Signs(nc, span, "ffn2", upT, downT, (st.norm.cent, st.norm.work))
            oproj_phase(nc, st, signs, att.rearrange("(t p) n -> p t n", p=P), x1, wo, x2)
            ffn_phase(nc, "ffn2", st, signs, False, x2, outT, None, 0, NCH, vecs)


def kernel(L0_attn_x, L0_attn_w_q, L0_attn_w_k, L0_attn_w_v, L0_attn_w_o, L0_ffn_up_weight, L0_ffn_down_weight,
           L0_ffn_up_scale, L0_ffn_down_scale, L0_ffn_output_scale):
    import numpy as np
    from concourse import bacc
    from concourse.bass_utils import run_bass_kernel_spmd

    def tiles(a):
        a = np.asarray(a)
        return np.ascontiguousarray(a.reshape(-1, P, a.shape[-1]).transpose(1, 0, 2))

    x = np.asarray(L0_attn_x)
    arrays = {
        "xT": tiles(x.reshape(TOK, D).T),
        "w_qT": tiles(np.asarray(L0_attn_w_q).T),
        "w_kT": tiles(np.asarray(L0_attn_w_k).T),
        "w_vT": tiles(np.asarray(L0_attn_w_v).T),
        "w_oT": tiles(np.asarray(L0_attn_w_o).T),
        "upT": tiles(np.asarray(L0_ffn_up_weight).T),
        "downT": tiles(np.asarray(L0_ffn_down_weight).T),
        "up_scale": np.ascontiguousarray(np.asarray(L0_ffn_up_scale).reshape(HT, P).T),
        "down_scale": np.ascontiguousarray(np.asarray(L0_ffn_down_scale).reshape(DT, P).T),
        "output_scale": np.ascontiguousarray(np.broadcast_to(np.asarray(L0_ffn_output_scale).reshape(1, 1), (P, 1))),
    }
    nc = bacc.Bacc("TRN2", target_bir_lowering=False, num_devices=1)
    args = [nc.dram_tensor(n, a.shape, mybir.dt.from_np(a.dtype), kind="ExternalInput").ap() for n, a in arrays.items()]
    out = nc.dram_tensor("outT", (P, DT, TOK), F32, kind="ExternalOutput").ap()
    macaron_kernel(nc, *args, out)
    r = run_bass_kernel_spmd(nc, [arrays], core_ids=[0])
    got = np.asarray(r.results[0]["outT"])
    return np.ascontiguousarray(got.transpose(1, 0, 2).reshape(D, TOK).T).reshape(BATCH, SEQ, D)
```

```python
import concourse.bass as bass
from concourse import mybir
from contextlib import ExitStack

F32 = mybir.dt.float32
F32R = mybir.dt.float32r
ALU = mybir.AluOpType
ACT = mybir.ActivationFunctionType
AX = mybir.AxisListType

P = 128
BATCH, SEQ, D, HID = 2, 2048, 512, 2048
TOK = BATCH * SEQ
HEADS, HD = 16, 32
SCALE = 1.0 / HD ** 0.5
EPS = 1e-5
CH = 512
NCH = TOK // CH
DT = D // P
HT = HID // P
KT = SEQ // P
QC = SEQ // CH
NH = BATCH * HEADS

PARTS3 = ((0, 0), (0, 1), (1, 0))


def f32(ap):
    return ap.bitcast(F32)


NV, NA = 18, 4
CENT_READ = 16
HALF = (slice(0, DT // 2), slice(DT // 2, DT))


class Norm:
    def __init__(self, nc, ctx, tag, ones_mean):
        def sb(n, shape, dt=F32):
            return ctx.enter_context(nc.sbuf_tensor(f"{tag}_{n}", shape, dt))
        self.nc, self.ones = nc, ones_mean
        self.pair = sb("pair", [P, 2, CH])
        self.sum = sb("sum", [P, CH])
        self.sum_hi, self.sum_lo = sb("sum_hi", [P, CH], F32R), sb("sum_lo", [P, CH], F32R)
        self.var, self.std = sb("var", [P, CH]), sb("std", [P, CH])
        self.inv, self.tmp = sb("inv", [P, CH]), sb("tmp", [P, CH])
        self.cent = sb("cent", [P, DT, CH])
        self.work = sb("work", [P, DT, CH])
        self.mean_ps = ctx.enter_context(nc.psum_tensor(f"{tag}_mean", [P, CH], F32))
        self.var_ps = ctx.enter_context(nc.psum_tensor(f"{tag}_varps", [P, CH], F32))
        self.dve = ctx.enter_context(nc.semaphore(f"{tag}_norm_dve"))
        self.act = ctx.enter_context(nc.semaphore(f"{tag}_norm_act"))
        self.pe = ctx.enter_context(nc.semaphore(f"{tag}_norm_pe"))

    def vector(self, dve, k, m, x, lo, hi):
        nc = self.nc
        if k not in (0, 4, 5, 9, 10, 15, 16, 17):
            dve.wait_ge(self.dve, m * NV + k)
        if k == 0:
            ins = nc.vector.tensor_tensor(self.pair[:], x[:, 0:2, :], x[:, 2:4, :], ALU.add)
        elif k == 1:
            ins = nc.vector.tensor_tensor(self.sum[:], self.pair[:, 0, :], self.pair[:, 1, :], ALU.add)
        elif k == 2:
            ins = nc.vector.tensor_copy(self.sum_hi[:], self.sum[:])
        elif k == 3:
            ins = nc.vector.tensor_tensor(self.sum_lo[:], self.sum[:], f32(self.sum_hi[:]), ALU.subtract)
        elif k == 4:
            dve.wait_ge(self.pe, m * 2 + 1)
            mean = self.mean_ps[:].unsqueeze(1).to_broadcast([P, DT, CH])
            ins = nc.vector.tensor_tensor(self.cent[:], x, mean, ALU.subtract)
        elif k == 5:
            dve.wait_ge(self.act, m * NA + 1)
            ins = nc.vector.tensor_tensor(self.pair[:], self.work[:, 0:2, :], self.work[:, 2:4, :], ALU.add)
        elif k == 6:
            ins = nc.vector.tensor_tensor(self.sum[:], self.pair[:, 0, :], self.pair[:, 1, :], ALU.add)
        elif k == 7:
            ins = nc.vector.tensor_copy(self.sum_hi[:], self.sum[:])
        elif k == 8:
            ins = nc.vector.tensor_tensor(self.sum_lo[:], self.sum[:], f32(self.sum_hi[:]), ALU.subtract)
        elif k == 9:
            dve.wait_ge(self.pe, m * 2 + 2)
            ins = nc.vector.tensor_scalar(self.var[:], self.var_ps[:], EPS, None, ALU.add)
        elif k == 10:
            dve.wait_ge(self.act, m * NA + 2)
            ins = nc.vector.reciprocal(self.inv[:], self.std[:])
        elif k == 11:
            ins = nc.vector.scalar_tensor_tensor(self.tmp[:], self.var[:], -0.5, self.inv[:], ALU.mult, ALU.mult)
        elif k == 12:
            ins = nc.vector.tensor_tensor(self.tmp[:], self.tmp[:], self.inv[:], ALU.mult)
        elif k == 13:
            ins = nc.vector.scalar_tensor_tensor(self.inv[:], self.tmp[:], 1.5, self.inv[:], ALU.add, ALU.mult)
        elif k in (14, 15):
            h = HALF[k - 14]
            inv = self.inv[:].unsqueeze(1).to_broadcast([P, DT // 2, CH])
            ins = nc.vector.tensor_tensor(self.work[:, h, :], self.cent[:, h, :], inv, ALU.mult)
        else:
            h = HALF[k - 16]
            dve.wait_ge(self.act, m * NA + k - 13)
            ins = nc.vector.tensor_tensor(lo[:, h, :], self.work[:, h, :], f32(hi[:, h, :]), ALU.subtract)
        ins.then_inc(self.dve, 1)

    def scalar(self, act, k, m, hi):
        nc = self.nc
        act.wait_ge(self.dve, m * NV + (5, 10, 15, 16)[k])
        if k == 0:
            ins = nc.scalar.activation(self.work[:], self.cent[:], ACT.Square)
        elif k == 1:
            ins = nc.scalar.activation(self.std[:], self.var[:], ACT.Sqrt)
        else:
            h = HALF[k - 2]
            ins = nc.scalar.activation(hi[:, h, :], self.work[:, h, :], ACT.Copy)
        ins.then_inc(self.act, 1)

    def tensor(self, pe, k, m):
        nc = self.nc
        pe.wait_ge(self.dve, m * NV + (4, 9)[k])
        out = (self.mean_ps, self.var_ps)[k]
        nc.tensor.matmul(out[:], self.ones[:], self.sum_hi[:], start=True, stop=False)
        nc.tensor.matmul(out[:], self.ones[:], self.sum_lo[:], start=False, stop=True).then_inc(self.pe, 1)


class Stream:

    def __init__(self, nc, ctx, tag, ones_mean):
        def sb(n, dt=F32):
            return ctx.enter_context(nc.sbuf_tensor(f"{tag}_{n}", [P, DT, CH], dt))
        self.x = [sb(f"x{i}") for i in range(2)]
        self.out = sb("out")
        self.hi = [sb(f"hi{i}", F32R) for i in range(2)]
        self.lo = [sb(f"lo{i}", F32R) for i in range(2)]
        self.norm = Norm(nc, ctx, tag, ones_mean)
        self.loaded = [ctx.enter_context(nc.semaphore(f"{tag}_loaded{i}")) for i in range(2)]
        self.stored = ctx.enter_context(nc.semaphore(f"{tag}_stored"))

    def load(self, sp, j, src, n):
        sp.dma_start(self.x[j][:], chunk(src, n)).then_inc(self.loaded[j], 16)

    def vector_norm(self, dve, k, m, j):
        self.norm.vector(dve, k, m, self.x[j][:], self.lo[j][:], self.hi[j][:])

    def scalar_norm(self, act, k, m, j):
        self.norm.scalar(act, k, m, self.hi[j][:])


class Signs:

    def __init__(self, nc, ctx, tag, up_raw, down_raw, stages):
        self.nc, self.up_raw, self.down_raw, self.stages = nc, up_raw, down_raw, stages
        self.up = ctx.enter_context(nc.sbuf_tensor(f"{tag}_up_w", [P, DT, HID], F32R))
        self.down = ctx.enter_context(nc.sbuf_tensor(f"{tag}_down_w", [P, HT, D], F32R))
        self.loaded = [ctx.enter_context(nc.semaphore(f"{tag}_sign_loaded{i}")) for i in range(2)]
        self.made = ctx.enter_context(nc.semaphore(f"{tag}_sign_made"))

    def stage(self, q):
        return self.stages[q % 2][:].rearrange("p a b -> p (a b)")

    def load(self, sp, q):
        if q >= 2:
            sp.wait_ge(self.made, q - 1)
        src = self.up_raw[:, q, :] if q < 4 else self.down_raw[:, 4 * (q - 4):4 * (q - 3), :].rearrange("p a b -> p (a b)")
        sp.dma_start(self.stage(q), src).then_inc(self.loaded[q % 2], 16)

    def make(self, act, q):
        act.wait_ge(self.loaded[q % 2], 16 * (q // 2 + 1))
        dst = self.up[:, q, :] if q < 4 else self.down[:, 4 * (q - 4):4 * (q - 3), :].rearrange("p a b -> p (a b)")
        self.nc.scalar.activation(dst, self.stage(q), ACT.Sign).then_inc(self.made, 1)


class HeadOut:

    def __init__(self, nc, ctx, att, sums_scr, inv_scr):
        def sb(n, shape):
            return ctx.enter_context(nc.sbuf_tensor(f"head_{n}", shape, F32))
        self.nc, self.att, self.sums_scr, self.inv_scr = nc, att, sums_scr, inv_scr
        self.raw, self.total = sb("raw", [P, CH]), sb("total", [P, CH])
        self.tot_t, self.inv_t = sb("tot_t", [P, KT]), sb("inv_t", [P, KT])
        self.inv_b, self.fin = sb("inv_b", [P, CH]), sb("fin", [P, CH])
        self.copied = ctx.enter_context(nc.semaphore("head_copied"))
        self.moved = ctx.enter_context(nc.semaphore("head_moved"))
        self.divided = ctx.enter_context(nc.semaphore("head_divided"))

    def move(self, eng, H, row, col):
        eng.wait_ge(self.copied, 2 * H + 2)
        eng.dma_start(self.sums_scr[:, :], self.total[0:P:HD, :]).then_inc(self.moved, 16)
        eng.wait_ge(self.moved, PER_HEAD * H + 16)
        eng.dma_start(self.tot_t[:], self.sums_scr.rearrange("a (b c) -> (a b) c", c=KT)).then_inc(self.moved, 16)
        eng.wait_ge(self.divided, 2 * H + 1)
        eng.dma_start(self.inv_scr.rearrange("a (b c) -> (a b) c", c=KT), self.inv_t[:]).then_inc(self.moved, 16)
        eng.wait_ge(self.moved, PER_HEAD * H + 48)
        for c in range(QC):
            eng.dma_start(self.inv_b[c * HD:(c + 1) * HD, :], self.inv_scr[c:c + 1, :].to_broadcast([HD, CH])).then_inc(self.moved, 16)
        eng.wait_ge(self.divided, 2 * H + 2)
        for c in range(QC):
            eng.dma_start(self.att[bass.ds(row, HD), bass.ds(col + c * CH, CH)], self.fin[c * HD:(c + 1) * HD, :]).then_inc(self.moved, 16)

    def invert(self, dve, H):
        dve.wait_ge(self.moved, PER_HEAD * H + 32)
        self.nc.vector.reciprocal(self.inv_t[:], self.tot_t[:]).then_inc(self.divided, 1)

    def scale(self, dve, H):
        dve.wait_ge(self.moved, PER_HEAD * H + 48 + 16 * QC)
        self.nc.vector.tensor_tensor(self.fin[:], self.raw[:], self.inv_b[:], ALU.mult).then_inc(self.divided, 1)


PER_HEAD = (3 + 2 * QC) * 16


class OProj:

    def __init__(self, nc, ctx, st, att, wo, head_out):
        self.nc, self.st, self.att, self.wo, self.head_out = nc, st, att, wo, head_out
        self.loaded = ctx.enter_context(nc.semaphore("op_loaded"))
        self.hi_done = ctx.enter_context(nc.semaphore("op_hi_done"))
        self.lo_done = ctx.enter_context(nc.semaphore("op_lo_done"))
        self.ready = ctx.enter_context(nc.semaphore("op_ready"))
        self.added = ctx.enter_context(nc.semaphore("op_added"))

    def bank(self, t):
        return (self.st.norm.mean_ps, self.st.norm.var_ps)[t % 2]

    def load(self, sp, m):
        sp.dma_start(self.st.norm.cent[:], chunk(self.att, m)).then_inc(self.loaded, 16)

    def split_hi(self, act, m, j):
        act.wait_ge(self.loaded, 16 * (m + 1))
        self.nc.scalar.activation(self.st.hi[j][:], self.st.norm.cent[:], ACT.Copy).then_inc(self.hi_done, 1)

    def split_lo(self, dve, m, j):
        dve.wait_ge(self.hi_done, m + 1)
        self.nc.vector.tensor_tensor(self.st.lo[j][:], self.st.norm.cent[:], f32(self.st.hi[j][:]),
                                     ALU.subtract).then_inc(self.lo_done, 1)

    def product(self, pe, m, j, t):
        if t == 0:
            pe.wait_ge(self.lo_done, m + 1)
        if t >= 2:
            pe.wait_ge(self.added, DT * m + t - 1)
        parts = (self.st.hi[j], self.st.lo[j])
        for dt in range(DT):
            for p, q in PARTS3:
                ins = self.nc.tensor.matmul(self.bank(t)[:], self.wo[p][:, dt, t * P:(t + 1) * P], parts[q][:, dt, :],
                                            start=(dt == 0 and (p, q) == (0, 0)),
                                            stop=(dt == DT - 1 and (p, q) == (1, 0)))
        ins.then_inc(self.ready, 1)

    def add(self, dve, m, j, t):
        dve.wait_ge(self.ready, DT * m + t + 1)
        x = self.st.x[j][:, t, :]
        self.nc.vector.tensor_tensor(x, self.bank(t)[:], x, ALU.add).then_inc(self.added, 1)


def chunk(ap, n):
    return ap[:, :, bass.ds(n * CH, CH)]


def ffn_phase(nc, tag, st, signs, x_in, x_out, next_in, vecs, qkv_stage=None, oproj=None):
    with ExitStack() as ctx:
        def sb(n, shape, dt=F32):
            return ctx.enter_context(nc.sbuf_tensor(f"{tag}_{n}", shape, dt))

        def ps(n):
            return ctx.enter_context(nc.psum_tensor(f"{tag}_{n}", [P, CH], F32))

        def sem(n):
            return ctx.enter_context(nc.semaphore(f"{tag}_{n}"))

        RING, RAW = 4, 2
        hid_hi, hid_lo = sb("hid_hi", [P, RING, CH], F32R), sb("hid_lo", [P, RING, CH], F32R)
        hid = sb("hid", [P, RAW, CH])
        norm, x, parts = st.norm, st.x, (st.hi, st.lo)
        up_ps = [ps(f"up{i}") for i in range(2)]
        down_ps = [ps(f"down{i}") for i in range(DT)]

        up_ready = sem("up_ready")
        up_read = sem("up_read")
        hid_ready = sem("hid_ready")
        hid_used = sem("hid_used")
        down_read = sem("down_read")
        out_stored = st.stored
        LAG = 3
        if oproj is None:
            DVE_AT = {3: (0, 1), 4: (2, 3), 6: (4,), 8: (5, 6), 9: (7, 8), 11: (9,), 12: (10,),
                      13: (11, 12), 14: (13, 14, 15), 15: (16, 17)}
            ACT_AT = {6: (0,), 11: (1,), 14: (2, 3)}
            PE_AT = {6: 0, 11: 1}
        else:
            DVE_AT = {6: (0, 1, 2, 3), 8: (4,), 9: (5, 6, 7, 8), 10: (9,), 11: (10,), 12: (11, 12, 13),
                      13: (14, 15), 15: (16, 17)}
            ACT_AT = {8: (0,), 11: (1,), 13: (2, 3)}
            PE_AT = {8: 0, 11: 1}
        ADD_AT = 2
        NP = NCH // 2

        with nc.Block() as block:
            def pairs(eng, body):
                with eng.Fori(0, NP - 1) as cp:
                    body(cp, False)
                body(NP - 1, True)

            def ahead(last, j):
                return next_in is not None or not (last and j)

            @block.sync
            def _(sp):
                sp.sem_inc(out_stored, 16)
                if oproj:
                    oproj.load(sp, 0)
                    st.load(sp, 0, x_in, 0)
                for q in range(2):
                    signs.load(sp, q)
                if oproj:
                    oproj.head_out.move(sp, NH - 1, (HEADS - 1) * HD, SEQ)
                for q in range(2, 8):
                    signs.load(sp, q)
                if oproj:
                    sp.wait_ge(norm.dve, CENT_READ)
                    oproj.load(sp, 1)
                sp.wait_ge(signs.made, 8)
                st.load(sp, 1, x_in, 1)
                if qkv_stage:
                    for w, raw in enumerate(qkv_stage["raw"]):
                        sp.dma_start(qkv_stage["buf"][:, w], raw).then_inc(qkv_stage["loaded"], 16)
                if oproj:
                    sp.wait_ge(oproj.head_out.moved, PER_HEAD * NH)

                def pair(cp, last):
                    for j in range(2):
                        n = 2 * cp + j
                        if oproj and not last:
                            sp.wait_ge(norm.dve, NV * (n + 1) + CENT_READ)
                            oproj.load(sp, n + 2)
                        sp.wait_ge(down_read, n + 2)
                        if not last:
                            st.load(sp, j, x_in, n + 2)
                        elif j == 0 and next_in is not None:
                            sp.wait_ge(out_stored, 32)
                            st.load(sp, 0, next_in, 0)
                        sp.dma_start(chunk(x_out, n), st.out[:]).then_inc(out_stored, 16)
                pairs(sp, pair)
                if next_in is None:
                    sp.wait_ge(out_stored, 16 * NCH + 16)

            @block.vector
            def _(dve):
                dve.sem_inc(hid_ready, RAW)
                dve.sem_inc(down_read, 1)
                if oproj:
                    oproj.split_lo(dve, 0, 0)
                dve.wait_ge(st.loaded[0], 16)
                if oproj:
                    for t in range(DT):
                        oproj.add(dve, 0, 0, t)
                        if t == 0:
                            oproj.head_out.invert(dve, NH - 1)
                    dve.wait_ge(oproj.added, DT)
                for k in range(NV):
                    st.vector_norm(dve, k, 0, 0)
                    if oproj and k == 3:
                        oproj.head_out.scale(dve, NH - 1)
                if oproj:
                    oproj.split_lo(dve, 1, 1)

                def pair(cp, last):
                    for j in range(2):
                        n = 2 * cp + j
                        for ht in range(HT):
                            dve.wait_ge(up_read, 2 + n * HT + ht + 1)
                            nc.vector.tensor_tensor(hid_lo[:, ht % RING, :], hid[:, ht % RAW, :],
                                                    f32(hid_hi[:, ht % RING, :]), ALU.subtract).then_inc(hid_ready, 1)
                            if ahead(last, j):
                                if ht == ADD_AT:
                                    dve.wait_ge(st.loaded[1 - j], 16 * (cp + j) + 16)
                                if oproj and ADD_AT <= ht < ADD_AT + DT:
                                    oproj.add(dve, n + 1, 1 - j, ht - ADD_AT)
                                if oproj and ht == ADD_AT + DT:
                                    dve.wait_ge(oproj.added, DT * (n + 2))
                                for k in DVE_AT.get(ht, ()):
                                    st.vector_norm(dve, k, n + 1, 1 - j)
                        if oproj and not last:
                            oproj.split_lo(dve, n + 2, j)
                        dve.wait_ge(hid_used, RING + n * HT + HT)
                        dve.wait_ge(out_stored, 16 * n + 16)
                        for dt in range(DT):
                            ins = nc.vector.scalar_tensor_tensor(st.out[:, dt, :], down_ps[dt][:], vecs["down"][:, dt:dt + 1],
                                                                 x[j][:, dt, :], ALU.mult, ALU.add)
                        ins.then_inc(down_read, 1)
                pairs(dve, pair)

            @block.scalar
            def _(act):
                act.sem_inc(up_read, 2)
                if oproj:
                    oproj.split_hi(act, 0, 0)
                made = 0
                for k, upto in enumerate((2, 3, 5, 5) if oproj else (1, 3, 5, 5)):
                    for q in range(made, upto):
                        signs.make(act, q)
                    st.scalar_norm(act, k, 0, 0)
                    made = upto
                for q in range(made, 8):
                    signs.make(act, q)
                if oproj:
                    oproj.split_hi(act, 1, 1)

                def pair(cp, last):
                    for j in range(2):
                        n = 2 * cp + j
                        for ht in range(HT):
                            act.wait_ge(up_ready, n * HT + ht + 1)
                            act.wait_ge(hid_ready, n * HT + ht + 1)
                            nc.scalar.activation(hid[:, ht % RAW, :], up_ps[ht % 2][:], ACT.Relu,
                                                 scale=vecs["up"][:, ht:ht + 1])
                            act.wait_ge(hid_used, n * HT + ht + 1)
                            nc.scalar.activation(hid_hi[:, ht % RING, :], up_ps[ht % 2][:], ACT.Relu,
                                                 scale=vecs["up"][:, ht:ht + 1]).then_inc(up_read, 1)
                            if ahead(last, j):
                                for k in ACT_AT.get(ht, ()):
                                    st.scalar_norm(act, k, n + 1, 1 - j)
                        if oproj and not last:
                            oproj.split_hi(act, n + 2, j)
                pairs(act, pair)

            @block.tensor
            def _(pe):
                pe.sem_inc(hid_used, RING)
                if oproj:
                    for t in range(DT):
                        oproj.product(pe, 0, 0, t)
                norm.tensor(pe, 0, 0)
                norm.tensor(pe, 1, 0)
                pe.wait_ge(signs.made, 4)

                def pair(cp, last):
                    for j in range(2):
                        n = 2 * cp + j
                        pe.wait_ge(norm.dve, NV * (n + 1))
                        for ht in range(HT + LAG):
                            if ht < HT:
                                pe.wait_ge(up_read, n * HT + ht + 1)
                                for dt in range(DT):
                                    for i, part in enumerate(parts):
                                        ins = nc.tensor.matmul(up_ps[ht % 2][:], signs.up[:, dt, ht * P:(ht + 1) * P],
                                                               part[j][:, dt, :], start=(dt == 0 and i == 0),
                                                               stop=(dt == DT - 1 and i == 1))
                                ins.then_inc(up_ready, 1)
                            if oproj and ADD_AT <= ht < ADD_AT + DT and ahead(last, j):
                                oproj.product(pe, n + 1, 1 - j, ht - ADD_AT)
                            if ht in PE_AT and not oproj and ahead(last, j):
                                norm.tensor(pe, PE_AT[ht], n + 1)
                            h = ht - LAG
                            if h >= 0:
                                if h == 0:
                                    pe.wait_ge(down_read, n + 1)
                                if h % 4 == 0:
                                    pe.wait_ge(signs.made, 5 + h // 4)
                                pe.wait_ge(hid_ready, RAW + n * HT + h + 1)
                                for dt in range(DT):
                                    for i, part in enumerate((hid_hi, hid_lo)):
                                        ins = nc.tensor.matmul(down_ps[dt][:], signs.down[:, h, dt * P:(dt + 1) * P],
                                                               part[:, h % RING, :], start=(h == 0 and i == 0),
                                                               stop=(h == HT - 1 and i == 1))
                                ins.then_inc(hid_used, 1)
                            if ht in PE_AT and oproj and ahead(last, j):
                                norm.tensor(pe, PE_AT[ht], n + 1)
                pairs(pe, pair)


def qkv_phase(nc, st, x_in, m0, l0, w_st, w_loaded, qk_parts, v_scr):
    with ExitStack() as ctx:
        def sb(n, shape, dt=F32):
            return ctx.enter_context(nc.sbuf_tensor(f"qkv_{n}", shape, dt))

        def sem(n):
            return ctx.enter_context(nc.semaphore(f"qkv_{n}"))

        w_hi, w_lo = sb("w_hi", [P, 3, DT, D], F32R), sb("w_lo", [P, 3, DT, D], F32R)
        norm, xh, xl = st.norm, st.hi, st.lo
        RING = 4
        o_hi, o_lo = sb("o_hi", [P, RING, CH], F32R), sb("o_lo", [P, RING, CH], F32R)
        o_v = sb("o_v", [P, RING, CH])
        out_ps = [ctx.enter_context(nc.psum_tensor(f"qkv_o{i}", [P, CH], F32)) for i in range(RING)]
        w_rounded, w_split = sem("w_rounded"), sem("w_split")
        out_ready = sem("out_ready")
        act_read = sem("act_read")
        out_read = sem("out_read")
        stored = [sem(f"stored{i}") for i in range(RING)]
        NT = 12
        PER = 80
        W_PARTS = [(slice(None), 0, slice(None), slice(i * P, (i + 1) * P)) for i in range(DT)] + [(slice(None), w) for w in (1, 2)]
        BEFORE = (16, 48, 80)

        with nc.Block() as block:
            @block.sync
            def _(sp):
                for s in range(RING):
                    sp.sem_inc(stored[s], 16)
                sp.wait_ge(st.stored, 16 * 2 + 16)
                st.load(sp, 1, x_in, 1)
                sp.wait_ge(st.stored, 16 * NCH + 16)

                def pair(cp, last):
                    for j in range(2):
                        n = 2 * cp + j
                        if not last:
                            sp.wait_ge(norm.dve, NV * (n + 1 + m0))
                            st.load(sp, j, x_in, n + 2)
                        for t in range(NT):
                            sp.wait_ge(out_read, RING + n * NT + t + 1)
                            s = t % RING
                            if t < 8:
                                rows = slice((t % 4) * P, (t % 4 + 1) * P)
                                for part, src in ((0, o_hi), (1, o_lo)):
                                    dst = qk_parts[t // 4][part][rows, bass.ds(n * CH, CH)]
                                    sp.dma_start(dst, f32(src[:, s, :])).then_inc(stored[s], 16)
                            else:
                                sp.dma_start(v_scr[bass.ds(n * CH + (t - 8) * P, P), :], o_v[:, s, :]).then_inc(stored[s], 16)
                with sp.Fori(0, NCH // 2 - 1) as cp:
                    pair(cp, False)
                pair(NCH // 2 - 1, True)
                for s in range(RING):
                    sp.wait_ge(stored[s], PER * NCH + 16)

            DVE_AT = {-1: (0, 1, 2, 3), 1: (4,), 2: (5, 6, 7, 8), 5: (9,), 6: (10, 11, 12, 13, 14, 15), 8: (16, 17)}
            ACT_AT = {1: (0,), 5: (1,), 7: (2, 3)}
            PE_AT = {1: 0, 5: 1}

            @block.vector
            def _(dve):
                dve.sem_inc(out_read, RING)
                for i, part in enumerate(W_PARTS):
                    dve.wait_ge(w_rounded, i + 1)
                    nc.vector.tensor_tensor(w_lo[part], w_st[part], f32(w_hi[part]), ALU.subtract).then_inc(w_split, 1)

                def pair(cp, last):
                    for j in range(2):
                        n = 2 * cp + j
                        if not (last and j):
                            dve.wait_ge(st.loaded[1 - j], 16 * (cp + j) + 16 + 8 * l0)
                            for k in DVE_AT[-1]:
                                st.vector_norm(dve, k, n + 1 + m0, 1 - j)
                        for t in range(NT):
                            s = t % RING
                            if t < 8:
                                dve.wait_ge(act_read, n * 8 + t + 1)
                                nc.vector.tensor_tensor(o_lo[:, s, :], out_ps[s][:], f32(o_hi[:, s, :]),
                                                        ALU.subtract).then_inc(out_read, 1)
                            else:
                                dve.wait_ge(stored[s], n * PER + BEFORE[2])
                                dve.wait_ge(out_ready, n * NT + t + 1)
                                nc.vector.tensor_copy(o_v[:, s, :], out_ps[s][:]).then_inc(out_read, 1)
                            if not (last and j):
                                for k in DVE_AT.get(t, ()):
                                    st.vector_norm(dve, k, n + 1 + m0, 1 - j)
                with dve.Fori(0, NCH // 2 - 1) as cp:
                    pair(cp, False)
                pair(NCH // 2 - 1, True)

            @block.scalar
            def _(act):
                act.wait_ge(w_loaded, 48)
                for part in W_PARTS:
                    nc.scalar.activation(w_hi[part], w_st[part], ACT.Copy).then_inc(w_rounded, 1)

                def pair(cp, last):
                    for j in range(2):
                        n = 2 * cp + j
                        for t in range(NT):
                            s = t % RING
                            if t < 8:
                                act.wait_ge(stored[s], n * PER + BEFORE[t // 4])
                                act.wait_ge(out_ready, n * NT + t + 1)
                                nc.scalar.activation(o_hi[:, s, :], out_ps[s][:], ACT.Copy).then_inc(act_read, 1)
                            if not (last and j):
                                for k in ACT_AT.get(t, ()):
                                    st.scalar_norm(act, k, n + 1 + m0, 1 - j)
                with act.Fori(0, NCH // 2 - 1) as cp:
                    pair(cp, False)
                pair(NCH // 2 - 1, True)

            @block.tensor
            def _(pe):
                w = (w_hi, w_lo)

                def pair(cp, last):
                    for j in range(2):
                        n = 2 * cp + j
                        act_parts = (xh[j], xl[j])
                        pe.wait_ge(norm.dve, NV * (n + 1 + m0))
                        for t in range(NT):
                            which, i = t // 4, t % 4
                            if which == 0 or i == 0:
                                pe.wait_ge(w_split, i + 1 if which == 0 else DT + which)
                            pe.wait_ge(out_read, n * NT + t + 1)
                            for dt in range(DT):
                                for a, b in PARTS3:
                                    if which < 2:
                                        left, right = w[a][:, which, dt, i * P:(i + 1) * P], act_parts[b][:, dt, :]
                                    else:
                                        left, right = act_parts[b][:, dt, i * P:(i + 1) * P], w[a][:, which, dt, :]
                                    ins = nc.tensor.matmul(out_ps[t % RING][:], left, right,
                                                           start=(dt == 0 and (a, b) == (0, 0)),
                                                           stop=(dt == DT - 1 and (a, b) == (1, 0)))
                            ins.then_inc(out_ready, 1)
                            if t in PE_AT and not (last and j):
                                norm.tensor(pe, PE_AT[t], n + 1 + m0)
                with pe.Fori(0, NCH // 2 - 1) as cp:
                    pair(cp, False)
                pair(NCH // 2 - 1, True)


def bank_order(units, banks, second):
    ages, bank = list(range(banks)), []
    for i in range(units):
        b = ages.pop(1 if i in second else 0)
        ages.append(b)
        bank.append(b)
    assert ages == list(range(banks))
    last = {b: u - units for u, b in enumerate(bank)}
    freed = []
    for i, b in enumerate(bank):
        freed.append(last[b] + 1)
        last[b] = i
    return bank, freed


def attention_phase(nc, qk_parts, v_scr, head_out, ident, ones_sum, wo_raw, wo):
    NB = 4
    KQ, KM = 3 * HD, 3 * HD + 2
    LEAD, LAG = 4, 2
    PR = 8
    SR, MR = 3, 3
    UNITS = KT * QC
    S_BANK, S_FREED = bank_order(UNITS, SR, (23, 46))
    M_BANK, M_FREED = bank_order(UNITS, MR, (22, 51))
    POOLED = (0, 1, 2, 4, 5, 7, 8, 10, 11, 13, 14)
    UNPOOLED = 3
    NA_ = len(POOLED) - 1
    PER = 7 * 16
    with ExitStack() as ctx:
        def sb(n, shape, dt=F32):
            return ctx.enter_context(nc.sbuf_tensor(f"att_{n}", shape, dt))

        def ps(n):
            return ctx.enter_context(nc.psum_tensor(f"att_{n}", [P, CH], F32))

        def sem(n):
            return ctx.enter_context(nc.semaphore(f"att_{n}"))

        q_st = [sb(f"q{i}", [P, SEQ], F32R) for i in range(NB)]
        k_st = [sb(f"k{i}", [P, SEQ], F32R) for i in range(NB)]
        v_st = [sb(f"v{i}", [P, KT, HD]) for i in range(NB)]
        prob = [sb(f"p{i}", [P, SEQ]) for i in range(PR)]
        acc = [sb(f"acc{i}", [P, SEQ]) for i in range(2)]
        row_max = [sb(f"row_max{i}", [P, KT, QC]) for i in range(2)]
        neg_max = sb("neg_max", [P, KT])
        neg_parts = sb("neg_parts", [P, 2, KT], F32R)
        neg_rows = sb("neg_rows", [2 * KT, P], F32R)
        s_ps = [ps(f"s{i}") for i in range(SR)]
        m_ps = [ps(f"m{i}") for i in range(MR)]
        o_ps, t_ps = ps("o"), ps("t")

        loaded = [sem(f"loaded{i}") for i in range(NB)]
        ones_set = sem("ones_set")
        m_ready, m_read = sem("m_ready"), sem("m_read")
        neg_dve, neg_pe = sem("neg_dve"), sem("neg_pe")
        neg_loaded = sem("neg_loaded")
        s_ready, exp_done = sem("s_ready"), sem("exp_done")
        p_used = sem("p_used")
        summed = sem("summed")
        t_ready = sem("t_ready")
        TURN = KT - LEAD + 1
        t_bank = m_ps[M_BANK[QC + 2]]
        wo_loaded, wo_done = sem("wo_loaded"), sem("wo_done")

        def adds_before(kt):
            return max(1, POOLED.index(kt))

        with nc.Block() as block:
            def groups(eng, body):
                body(0, True, False)
                with eng.Fori(1, NH // NB - 1) as g:
                    body(g, False, False)
                body(NH // NB - 1, False, True)

            @block.sync
            def _(sp):
                def load(b, row, col):
                    for which, st in ((0, q_st[b]), (1, k_st[b])):
                        for i, part in enumerate(((0, 0, 1), (0, 1, 0))[which]):
                            sp.dma_start(f32(st[i * HD:(i + 1) * HD, :]),
                                         qk_parts[which][part][bass.ds(row, HD), bass.ds(col, SEQ)]).then_inc(loaded[b], 16)
                    sp.dma_start(v_st[b][:], v_scr[bass.ds(col, SEQ), bass.ds(row, HD)].rearrange("(t p) d -> p t d", p=P)
                                 ).then_inc(loaded[b], 16)

                def max_rows(b, H):
                    sp.wait_ge(neg_dve, 4 * H + 4)
                    for r in range(2):
                        sp.dma_start(f32(q_st[b][KQ + r:KQ + r + 1, :].rearrange("o (t p) -> o t p", p=P)),
                                     f32(neg_rows[r * KT:(r + 1) * KT, :])).then_inc(neg_loaded, 16)

                for b in range(3):
                    load(b, b * HD, 0)
                sp.dma_start(prob[PR - 1][:], wo_raw.rearrange("p a b -> p (a b)")).then_inc(wo_loaded, 16)
                max_rows(0, 0)

                def body(g, first, last):
                    for j in range(NB):
                        H = NB * g + j
                        if not (last and j):
                            sp.wait_ge(s_ready, UNITS * H)
                            sp.wait_ge(p_used, PR + KT * H)
                            X = H + 3
                            load((j + 3) % NB, X % HEADS * HD, X // HEADS * SEQ)
                        if not (first and j == 0):
                            Y = H - 1
                            head_out.move(sp, Y, Y % HEADS * HD, Y // HEADS * SEQ)
                        if not (last and j == NB - 1):
                            max_rows((j + 1) % NB, H + 1)
                groups(sp, body)
                sp.wait_ge(head_out.moved, PER_HEAD * (NH - 1))

            @block.gpsimd
            def _(pool):
                for b in range(NB):
                    nc.gpsimd.memset(f32(k_st[b][KQ:KM, :]), 1.0).then_inc(ones_set, 1)
                pool.sem_inc(summed, NA_)
                pool.wait_ge(ones_set, NB)
                pool.wait_ge(wo_done, 1)
                nc.gpsimd.tensor_tensor(wo[1][:].rearrange("p a b -> p (a b)"), prob[PR - 1][:],
                                        f32(wo[0][:].rearrange("p a b -> p (a b)")), ALU.subtract).then_inc(wo_done, 1)

                def body(g, first, last):
                    for j in range(NB):
                        H = NB * g + j
                        for i, kt in enumerate(POOLED):
                            if i == 0:
                                continue
                            pool.wait_ge(exp_done, SR + UNITS * H + QC * (kt + 1))
                            if i == 1:
                                if not (first and j < 2):
                                    pool.wait_ge(t_ready, H - 1)
                                a = prob[POOLED[0] % PR]
                            else:
                                pool.wait_ge(summed, NA_ * (H + 1) + i - 1)
                                a = acc[j % 2]
                            nc.gpsimd.tensor_tensor(acc[j % 2][:], a[:], prob[kt % PR][:], ALU.add).then_inc(summed, 1)
                groups(pool, body)

            @block.vector
            def _(dve):
                dve.sem_inc(m_read, MR)

                def reduce_tile(T, odd, qt, chunks=range(QC)):
                    for c in chunks:
                        dve.wait_ge(m_ready, QC * T + c + 1)
                        nc.vector.tensor_reduce(row_max[odd][:, qt, c:c + 1], m_ps[M_BANK[qt * QC + c]][:], axis=AX.X, op=ALU.max).then_inc(m_read, 1)

                def negate(step, T_end, odd, h):
                    if step == 0:
                        dve.wait_ge(m_read, MR + QC * T_end)
                        nc.vector.tensor_reduce(neg_max[:], row_max[odd][:], axis=AX.X, op=ALU.max, negate=True).then_inc(neg_dve, 1)
                        return
                    dve.wait_ge(neg_dve, 4 * h + step)
                    if step == 1:
                        nc.vector.tensor_copy(neg_parts[:, 0, :], neg_max[:]).then_inc(neg_dve, 1)
                    else:
                        nc.vector.tensor_tensor(neg_parts[:, 1, :], neg_max[:], f32(neg_parts[:, 0, :]), ALU.subtract).then_inc(neg_dve, 1)

                def rows_out(h, wait):
                    dve.wait_ge(neg_pe, h + 1)
                    if wait:
                        dve.wait_ge(neg_loaded, 32 * h)
                    nc.vector.tensor_copy(neg_rows[:], t_bank[0:2 * KT, 0:P]).then_inc(neg_dve, 1)

                for qt in range(KT):
                    reduce_tile(qt, 0, qt)
                for step in range(3):
                    negate(step, KT, 0, 0)
                rows_out(0, False)
                for qt in range(LEAD):
                    reduce_tile(KT + qt, 1, qt)

                def body(g, first, last):
                    for j in range(NB):
                        H = NB * g + j
                        for kt in range(KT):
                            step_max = not (last and (j == NB - 1 or (j == NB - 2 and kt + LEAD >= KT)))
                            qt = (kt + LEAD) % KT
                            odd = (j + 1 + (kt + LEAD) // KT) % 2
                            if kt == TURN:
                                if step_max:
                                    reduce_tile(KT * (H + 1) + kt + LEAD, odd, qt, (0, 1))
                                if not (last and j == NB - 1):
                                    rows_out(H + 1, True)
                                if step_max:
                                    reduce_tile(KT * (H + 1) + kt + LEAD, odd, qt, (2, 3))
                            elif kt == TURN - 1 and not (last and j == NB - 1):
                                negate(0, KT * (H + 2), (j + 1) % 2, H + 1)
                                for c in range(QC):
                                    if step_max:
                                        reduce_tile(KT * (H + 1) + kt + LEAD, odd, qt, (c,))
                                    if c < 2:
                                        negate(c + 1, KT * (H + 2), (j + 1) % 2, H + 1)
                            elif step_max:
                                reduce_tile(KT * (H + 1) + kt + LEAD, odd, qt)
                            if not (first and j == 0):
                                if kt == 7:
                                    head_out.invert(dve, H - 1)
                                if kt == 10:
                                    head_out.scale(dve, H - 1)
                groups(dve, body)

            @block.scalar
            def _(act):
                act.sem_inc(exp_done, SR)
                act.wait_ge(wo_loaded, 16)
                nc.scalar.activation(wo[0][:].rearrange("p a b -> p (a b)"), prob[PR - 1][:], ACT.Copy).then_inc(wo_done, 1)
                act.wait_ge(wo_done, 2)

                def copy_out(H):
                    act.wait_ge(p_used, PR + KT * H + KT)
                    if not isinstance(H, int) or H > 0:
                        act.wait_ge(head_out.divided, 2 * H)
                    nc.scalar.activation(head_out.raw[:], o_ps[:], ACT.Copy).then_inc(head_out.copied, 1)

                def copy_sums(H):
                    act.wait_ge(t_ready, H + 1)
                    if not isinstance(H, int) or H > 0:
                        act.wait_ge(head_out.moved, PER_HEAD * (H - 1) + 32)
                    nc.scalar.activation(head_out.total[:], t_ps[:], ACT.Copy).then_inc(head_out.copied, 1)

                def body(g, first, last):
                    for j in range(NB):
                        H = NB * g + j
                        for kt in range(KT):
                            if not (first and j == 0):
                                if kt == LAG:
                                    copy_out(H - 1)
                                if kt == LAG + 2:
                                    copy_sums(H - 1)
                            act.wait_ge(p_used, KT * H + kt + 1)
                            old = (kt - PR) % KT
                            if old in POOLED:
                                h_old = H if kt >= PR else H - 1
                                act.wait_ge(summed, NA_ * (h_old + 1) + adds_before(old))
                            for c in range(QC):
                                act.wait_ge(s_ready, UNITS * H + QC * kt + c + 1)
                                nc.scalar.activation(prob[kt % PR][:, c * CH:(c + 1) * CH], s_ps[S_BANK[kt * QC + c]][:], ACT.Exp,
                                                     scale=SCALE).then_inc(exp_done, 1)
                groups(act, body)
                copy_out(NH - 1)
                copy_sums(NH - 1)

            @block.tensor
            def _(pe):
                pe.sem_inc(p_used, PR)
                pe.wait_ge(ones_set, NB)

                def maxima(b, T, qt, c):
                    i = qt * QC + c
                    pe.wait_ge(m_read, MR + QC * (T - qt) + M_FREED[i])
                    nc.tensor.matmul(m_ps[M_BANK[i]][:], q_st[b][0:KQ, qt * P:(qt + 1) * P], k_st[b][0:KQ, c * CH:(c + 1) * CH],
                                     start=True, stop=True).then_inc(m_ready, 1)

                def transpose_max(h):
                    pe.wait_ge(neg_dve, 4 * h + 3)
                    nc.tensor.transpose(t_bank[0:2 * KT, 0:P], f32(neg_parts[:].rearrange("p a b -> p (a b)")),
                                        ident[:]).then_inc(neg_pe, 1)

                def out_tile(H, b, kt):
                    pe.wait_ge(exp_done, SR + UNITS * H + QC * (kt + 1))
                    if kt == 0 and not (isinstance(H, int) and H == 0):
                        pe.wait_ge(head_out.copied, 2 * H - 1)
                    for c in range(QC):
                        rows = slice(c * HD, (c + 1) * HD)
                        ins = nc.tensor.matmul(o_ps[rows, :], v_st[b][:, kt, :], prob[kt % PR][:, c * CH:(c + 1) * CH],
                                               start=(kt == 0), stop=(kt == KT - 1))
                    if kt not in POOLED:
                        if kt == UNPOOLED and not (isinstance(H, int) and H == 0):
                            pe.wait_ge(head_out.copied, 2 * H)
                        for c in range(QC):
                            rows = slice(c * HD, (c + 1) * HD)
                            ins = nc.tensor.matmul(t_ps[rows, :], ones_sum[:], prob[kt % PR][:, c * CH:(c + 1) * CH],
                                                   start=(kt == UNPOOLED), stop=False)
                    ins.then_inc(p_used, 1)

                def pooled_sums(H, b2):
                    pe.wait_ge(summed, NA_ * (H + 2))
                    for c in range(QC):
                        rows = slice(c * HD, (c + 1) * HD)
                        ins = nc.tensor.matmul(t_ps[rows, :], ones_sum[:], acc[b2][:, c * CH:(c + 1) * CH],
                                               start=False, stop=True)
                    ins.then_inc(t_ready, 1)

                pe.wait_ge(loaded[0], PER)
                for qt in range(KT):
                    for c in range(QC):
                        maxima(0, qt, qt, c)
                transpose_max(0)
                pe.wait_ge(loaded[1], PER)
                pe.wait_ge(neg_dve, 4)
                for qt in range(LEAD):
                    for c in range(QC):
                        maxima(1, KT + qt, qt, c)

                def body(g, first, last):
                    for j in range(NB):
                        H = NB * g + j
                        pe.wait_ge(neg_loaded, 32 * (H + 1))
                        for kt in range(KT):
                            step_max = not (last and (j == NB - 1 or (j == NB - 2 and kt + LEAD >= KT)))
                            b, qt = ((j + 1) % NB, kt + LEAD) if kt + LEAD < KT else ((j + 2) % NB, kt + LEAD - KT)
                            T = KT * (H + 1) + kt + LEAD
                            def scores(c):
                                i = kt * QC + c
                                pe.wait_ge(exp_done, SR + UNITS * H + S_FREED[i])
                                nc.tensor.matmul(s_ps[S_BANK[i]][:], k_st[j][0:KM, kt * P:(kt + 1) * P],
                                                 q_st[j][0:KM, c * CH:(c + 1) * CH], start=True, stop=True).then_inc(s_ready, 1)

                            if step_max and kt == KT - LEAD:
                                pe.wait_ge(loaded[b], PER * (g + 1 + (j + 2) // NB))
                            for c in (0, 1):
                                scores(c)
                                if step_max:
                                    maxima(b, T, qt, c)
                            if kt == TURN and not (last and j == NB - 1):
                                if step_max:
                                    pe.wait_ge(m_read, MR + UNITS * (H + 2) + M_FREED[QC + 2])
                                transpose_max(H + 1)
                            if kt >= LAG:
                                out_tile(H, j, kt - LAG)
                            elif not (first and j == 0):
                                out_tile(H - 1, (j - 1) % NB, KT + kt - LAG)
                            if kt == LAG + 1 and not (first and j == 0):
                                pooled_sums(H - 1, (j - 1) % 2)
                            for c in (2, 3):
                                scores(c)
                                if step_max:
                                    if kt == TURN and c == 2:
                                        pe.wait_ge(neg_dve, 4 * (H + 1) + 4)
                                    maxima(b, T, qt, c)
                groups(pe, body)
                for kt in range(KT - LAG, KT):
                    out_tile(NH - 1, NB - 1, kt)
                pooled_sums(NH - 1, (NH - 1) % 2)


def macaron_kernel(nc, xT, w_qT, w_kT, w_vT, w_oT, upT, downT, up_scale, down_scale, output_scale, outT):
    ctx = ExitStack()
    with ctx:
        def sb(n, shape, dt=F32):
            return ctx.enter_context(nc.sbuf_tensor(n, shape, dt))

        def dram(n, shape, dt=F32):
            return nc.dram_tensor(n, shape, dt, kind="Internal").ap()

        x1 = dram("x_after_ffn", [P, DT, TOK])
        qk_parts = [[dram(f"{n}_{part}", [D, TOK]) for part in ("hi", "lo")] for n in ("q", "k")]
        v_scr = dram("v_rows", [TOK, D])
        att = dram("attention_out", [D, TOK])
        sums_scr, inv_scr = dram("prob_sums", [QC, CH]), dram("prob_inverse", [QC, CH])

        ones_mean = sb("ones_mean", [P, P], F32R)
        ones_sum = sb("ones_sum", [P, HD])
        ident = sb("ident", [P, P])
        up_s, down_s, out_s = sb("up_s", [P, HT]), sb("down_s", [P, DT]), sb("out_s", [P, 1])
        vecs = {"up": up_s, "down": down_s}
        const_loaded = ctx.enter_context(nc.semaphore("const_loaded"))
        const_set = ctx.enter_context(nc.semaphore("const_set"))
        scale_set = ctx.enter_context(nc.semaphore("scale_set"))

        with ExitStack() as span:
            st = Stream(nc, span, "s1", ones_mean)
            with nc.Block() as block:
                @block.sync
                def _(sp):
                    st.load(sp, 0, xT, 0)
                    sp.dma_start(up_s[:], up_scale).then_inc(const_loaded, 16)
                    sp.dma_start(down_s[:], down_scale).then_inc(const_loaded, 16)
                    sp.dma_start(out_s[:], output_scale).then_inc(const_loaded, 16)

                @block.gpsimd
                def _(pool):
                    nc.gpsimd.memset(f32(ones_mean[:]), 1.0 / D)
                    nc.gpsimd.memset(ones_sum[:], 1.0)
                    nc.gpsimd.memset(ident[:], 0.0).then_inc(const_set, 1)
                    pool.wait_ge(const_set, 1)
                    nc.gpsimd.affine_select(out=ident[:], in_=ident[:], compare_op=ALU.not_equal, fill=1.0,
                                            base=0, pattern=[[-1, P]], channel_multiplier=1).then_inc(const_set, 1)

                @block.vector
                def _(dve):
                    dve.wait_ge(const_loaded, 48)
                    nc.vector.tensor_scalar(down_s[:], down_s[:], out_s[:, 0:1], 0.5, ALU.mult, ALU.mult).then_inc(scale_set, 1)
                    dve.wait_ge(scale_set, 1)
                    dve.wait_ge(const_set, 2)
            w_st = span.enter_context(nc.sbuf_tensor("qkv_raw", [P, 3, DT, D], F32))
            w_loaded = span.enter_context(nc.semaphore("qkv_raw_loaded"))
            with ExitStack() as part:
                signs = Signs(nc, part, "ffn1", upT, downT, (st.out, st.x[1]))
                ffn_phase(nc, "ffn1", st, signs, xT, x1, x1, vecs,
                          {"raw": (w_qT, w_kT, w_vT), "buf": w_st, "loaded": w_loaded})
            qkv_phase(nc, st, x1, NCH, NCH, w_st, w_loaded, qk_parts, v_scr)
        with ExitStack() as span:
            wo = [span.enter_context(nc.sbuf_tensor(f"wo_{part}", [P, DT, D], F32R)) for part in ("hi", "lo")]
            head_out = HeadOut(nc, span, att, sums_scr, inv_scr)
            attention_phase(nc, qk_parts, v_scr, head_out, ident, ones_sum, w_oT, wo)
            st = Stream(nc, span, "s2", ones_mean)
            oproj = OProj(nc, span, st, att.rearrange("(t p) n -> p t n", p=P), wo, head_out)
            signs = Signs(nc, span, "ffn2", upT, downT, (st.out, st.x[1]))
            ffn_phase(nc, "ffn2", st, signs, x1, outT, None, vecs, oproj=oproj)


def kernel(L0_attn_x, L0_attn_w_q, L0_attn_w_k, L0_attn_w_v, L0_attn_w_o, L0_ffn_up_weight, L0_ffn_down_weight,
           L0_ffn_up_scale, L0_ffn_down_scale, L0_ffn_output_scale):
    import numpy as np
    from concourse import bacc
    from concourse.bass_utils import run_bass_kernel_spmd

    def tiles(a):
        a = np.asarray(a)
        return np.ascontiguousarray(a.reshape(-1, P, a.shape[-1]).transpose(1, 0, 2))

    x = np.asarray(L0_attn_x)
    arrays = {
        "xT": tiles(x.reshape(TOK, D).T),
        "w_qT": tiles(np.asarray(L0_attn_w_q).T),
        "w_kT": tiles(np.asarray(L0_attn_w_k).T),
        "w_vT": tiles(np.asarray(L0_attn_w_v).T),
        "w_oT": tiles(np.asarray(L0_attn_w_o).T),
        "upT": tiles(np.asarray(L0_ffn_up_weight).T),
        "downT": tiles(np.asarray(L0_ffn_down_weight).T),
        "up_scale": np.ascontiguousarray(np.asarray(L0_ffn_up_scale).reshape(HT, P).T),
        "down_scale": np.ascontiguousarray(np.asarray(L0_ffn_down_scale).reshape(DT, P).T),
        "output_scale": np.ascontiguousarray(np.broadcast_to(np.asarray(L0_ffn_output_scale).reshape(1, 1), (P, 1))),
    }
    nc = bacc.Bacc("TRN2", target_bir_lowering=False, num_devices=1)
    args = [nc.dram_tensor(n, a.shape, mybir.dt.from_np(a.dtype), kind="ExternalInput").ap() for n, a in arrays.items()]
    out = nc.dram_tensor("outT", (P, DT, TOK), F32, kind="ExternalOutput").ap()
    macaron_kernel(nc, *args, out)
    r = run_bass_kernel_spmd(nc, [arrays], core_ids=[0])
    got = np.asarray(r.results[0]["outT"])
    return np.ascontiguousarray(got.transpose(1, 0, 2).reshape(D, TOK).T).reshape(BATCH, SEQ, D)
```
